# Optimizing a Trainium2 kernel written in Bass

```python
import numpy as np
import jax
import jax.numpy as jnp

def _softmax(x, axis=-1):
    return jax.nn.softmax(x, axis=axis)

def _gelu(x):
    return jax.nn.gelu(x, approximate=True)

def _silu(x):
    return jax.nn.silu(x)

def _sigmoid(x):
    return jax.nn.sigmoid(x)

def _layernorm(x, axis=-1, eps=1e-05):
    m = jnp.mean(x, axis=axis, keepdims=True)
    v = jnp.var(x, axis=axis, keepdims=True)
    return (x - m) / jnp.sqrt(v + eps)

def _scatter_add(tgt, idx, src, axis=0):
    return tgt.at[idx].add(src)

def _segment_sum(src, seg, n):
    return jax.ops.segment_sum(src, seg, n)
kernel_name = 'mk_gnn_preln_d1_gnn_r32_7c4d70'

def setup_inputs(seed: int=0):
    np.random.seed(seed)
    _w = jnp.asarray

    def _rec_inputs():
        import jax
        import jax.numpy as jnp
        _gk = jax.random.key(seed)
        x = -0.000202 + 1 * jax.random.normal(jax.random.fold_in(_gk, 1), (3125, 128), jnp.float32)
        _s = jax.random.randint(jax.random.fold_in(_gk, 2), (50000,), 0, 3125, jnp.int32)
        _d = jax.random.randint(jax.random.fold_in(_gk, 3), (50000,), 0, 3125, jnp.int32)
        _loop = jnp.arange(3125, dtype=jnp.int32)
        src = jnp.concatenate([_s, _d, _loop])
        dst = jnp.concatenate([_d, _s, _loop])
        _o = jnp.argsort(dst, stable=True)
        src = src[_o]
        dst = dst[_o]
        edge_attr_3 = -3.57403e-05 + 0.999761 * jax.random.normal(jax.random.fold_in(_gk, 12), (103125, 3), jnp.float32)
        return (x, src, dst, edge_attr_3)
    x, src, dst, edge_attr_3 = _rec_inputs()

    def _L0_gnn_setup():
        import jax, jax.numpy as jnp
        import numpy as np
        N_NODES = 50000
        N_EDGES = 50000
        IN_FEAT = 128
        INTER_DIM = 128
        OUT_FEAT = 128
        EDGE_DIM = 3
        LEAKY_SLOPE = 0.01
        key = jax.random.key(seed)
        k = jax.random.split(key, 7)
        h = jax.random.normal(k[0], (N_NODES, IN_FEAT), dtype=jnp.float32)
        edge_w = jax.random.normal(k[1], (N_EDGES, EDGE_DIM), dtype=jnp.float32)
        W1 = jax.random.normal(k[2], (INTER_DIM, IN_FEAT + EDGE_DIM), dtype=jnp.float32) * 0.1
        W2 = jax.random.normal(k[3], (OUT_FEAT, IN_FEAT + INTER_DIM), dtype=jnp.float32) * 0.1
        b2 = jax.random.normal(k[4], (OUT_FEAT,), dtype=jnp.float32) * 0.01
        src = jax.random.randint(k[5], (N_EDGES,), 0, N_NODES, dtype=jnp.int64) if jax.config.jax_enable_x64 else jax.random.randint(k[5], (N_EDGES,), 0, N_NODES, dtype=jnp.int32)
        dst = jax.random.randint(k[6], (N_EDGES,), 0, N_NODES, dtype=src.dtype)
        return {'h': h, 'edge_w': edge_w, 'W1': W1, 'W2': W2, 'b2': b2, 'src': src, 'dst': dst}
    _L0_gnn_all = _L0_gnn_setup()
    _L0_gnn_in = {k: v for k, v in _L0_gnn_all.items() if k in ('W1', 'W2', 'b2')}
    del _L0_gnn_all
    return {'x': x, 'src': src, 'dst': dst, 'edge_attr_3': edge_attr_3, 'L0_gnn_W1': _L0_gnn_in['W1'], 'L0_gnn_W2': _L0_gnn_in['W2'], 'L0_gnn_b2': _L0_gnn_in['b2']}

def reference(x, src, dst, edge_attr_3, L0_gnn_W1, L0_gnn_W2, L0_gnn_b2):
    import jax
    import jax.numpy as jnp

    def _L0_gnn_ref(h, edge_w, W1, W2, b2, src, dst):
        import jax, jax.numpy as jnp
        import numpy as np
        N_NODES = 50000
        N_EDGES = 50000
        IN_FEAT = 128
        INTER_DIM = 128
        OUT_FEAT = 128
        EDGE_DIM = 3
        LEAKY_SLOPE = 0.01
        n_nodes = h.shape[0]
        m = jnp.concatenate([h[src], edge_w], axis=1)
        t = jax.nn.leaky_relu(m @ W1.T, negative_slope=LEAKY_SLOPE)
        s = jax.ops.segment_sum(t, dst, num_segments=n_nodes)
        deg = jax.ops.segment_sum(jnp.ones((dst.shape[0],), dtype=h.dtype), dst, num_segments=n_nodes)
        h_N = s / jnp.maximum(deg, 1.0)[:, None]
        h_total = jnp.concatenate([h, h_N], axis=1)
        return jax.nn.relu(h_total @ W2.T + b2)
    h = jnp.maximum(_layernorm(x, axis=-1), 0.0)
    x = x + _L0_gnn_ref(h, edge_attr_3, L0_gnn_W1, L0_gnn_W2, L0_gnn_b2, src, dst)
    return x

_drawn_inputs = setup_inputs


def setup_inputs(seed=0):
    import zlib

    import numpy as np

    out = dict(_drawn_inputs(seed))
    spreads = {}
    factors = {'edge_attr_3': 4.252, 'L0_gnn_b2': 8.0}
    for name, (base, spread) in spreads.items():
        noise = np.random.default_rng([zlib.crc32(name.encode()), seed]).standard_normal(out[name].shape)
        drawn = base * np.exp(spread * noise) if base else spread * noise
        out[name] = jnp.asarray(drawn.astype(out[name].dtype))
    for name, factor in factors.items():
        out[name] = (out[name] * factor).astype(out[name].dtype)
    return out
```

```python
import numpy as np

P = 128
NODES, EDGES, EDIM = 3125, 103125, 3
F = 128
SLOPE, EPS = 0.01, 1e-5

TPG = 8
GROUP = TPG * P
GROUPS = -(-EDGES // GROUP)
LAST_STAGED = GROUPS + 1
KE = TPG * EDIM

TILES = -(-NODES // P)
FULL = NODES // P
REST = NODES - FULL * P
TPC = 5
CHUNKS = TILES // TPC
NPAD = TILES * P

WIN = 64
SHIFT = 6
assert NPAD >= NODES + 1 + WIN - 1
BANK = 512
SLOT_CREDIT = 2


def build(nc, x, src_cols, dst_cols, dst_rows, edge_rows, w1a, w1b, w2a, w2b, b2, proj, out):
    import concourse.bass as bass
    from concourse import mybir
    from contextlib import ExitStack

    fp32, i32 = mybir.dt.float32, mybir.dt.int32
    ALU, ACT, AX = mybir.AluOpType, mybir.ActivationFunctionType, mybir.AxisListType
    ds = bass.ds

    with ExitStack() as ctx:
        def sb(name, shape, dt=fp32):
            return ctx.enter_context(nc.sbuf_tensor(name, shape, dt))

        def sem(name):
            return ctx.enter_context(nc.semaphore(name))

        x_sb = sb("x_sb", [P, TILES, F])
        norm = sb("norm", [P, TILES, F])
        h_t = sb("h_t", [F, NPAD])
        p_sb = sb("p_sb", [P, TILES, F])
        u_sb = sb("u_sb", [P, TILES, F])
        stats = sb("stats", [P, TILES, 6])
        mv = sb("mv", [P, TILES, 2])
        std = sb("std", [P, TILES])
        rstd = sb("rstd", [P, TILES])
        eps = sb("eps", [P, 1])
        ident = sb("ident", [P, P])
        ones = sb("ones", [P, P])
        w1a_sb = sb("w1a_sb", [F, F])
        w2a_sb = sb("w2a_sb", [F, F])
        w2b_sb = sb("w2b_sb", [F, F])
        b2_sb = sb("b2_sb", [1, F])
        w1b_diag = sb("w1b_diag", [KE, TPG, F])
        src_sb = sb("src_sb", [P, (LAST_STAGED + 1) * TPG], i32)
        dst_i = sb("dst_i", [P, GROUPS * TPG], i32)
        dst_f = sb("dst_f", [P, GROUPS * TPG])
        dst_g = sb("dst_g", [GROUPS, GROUP], i32)
        span = sb("span", [GROUPS, 2], i32)
        trips = sb("trips", [GROUPS, 2], i32)
        meta = sb("meta", [1, GROUPS, 2], i32)
        columns = sb("columns", [P, NPAD])
        idx = sb("idx", [P, 2, TPG], i32)
        ring = sb("ring", [P, 2, TPG, F])
        edge_t = sb("edge_t", [KE, 2, P])
        z = sb("z", [P, 2, TPG, F])
        t_sb = sb("t_sb", [P, 2, TPG, F])
        hot = sb("hot", [P, 2, TPG, WIN])
        hot_n = sb("hot_n", [P, 2, WIN])
        hot_x = sb("hot_x", [P, TPG, WIN])
        hot_xn = sb("hot_xn", [P, WIN])
        sums = sb("sums", [F, 2, NPAD])
        count = sb("count", [F, 2, TPC * P])
        h_n = sb("h_n", [F, 2, TPC * P])
        res = sb("res", [P, TILES, F])

        ps = ctx.enter_context(nc.psum_tensor("ps", [P, 8, BANK], fp32))
        flat = ps[:, :, :].rearrange("p b c -> p (b c)")
        msg_ps = [flat[:, 0:2 * BANK], flat[:, 2 * BANK:4 * BANK]]
        sum_ps = [flat[:, 4 * BANK:4 * BANK + 2 * WIN], flat[:, 5 * BANK:5 * BANK + 2 * WIN]]
        sum_x = flat[:, 4 * BANK + 2 * P:4 * BANK + 2 * P + 2 * WIN]
        low_ps = flat[:, 6 * BANK:8 * BANK]
        wide = [flat[:, 2 * b * BANK:2 * b * BANK + TPC * P] for b in range(4)]

        x_in = [sem(f"x_in{c}") for c in range(CHUNKS)]
        rest_zero = sem("rest_zero")
        consts = sem("consts")
        diag_zero = sem("diag_zero")
        w_in = sem("w_in")
        diag_in = sem("diag_in")
        src_in, dst_in, dstg_in = sem("src_in"), sem("dst_in"), sem("dstg_in")
        stats_done, mv_done, std_done, rstd_done = sem("stats_done"), sem("mv_done"), sem("std_done"), sem("rstd_done")
        norm_done, turned, h_done = sem("norm_done"), sem("turned"), sem("h_done")
        proj_ps, proj_sb, proj_out = sem("proj_ps"), sem("proj_sb"), sem("proj_out")
        u_ps, u_done = sem("u_ps"), sem("u_done")
        span_done, dif_done, trips_done, meta_in, dstf_done = (
            sem("span_done"), sem("dif_done"), sem("trips_done"), sem("meta_in"), sem("dstf_done"))
        staged = sem("staged")
        pool_tick = sem("pool_tick")
        gathered = [sem("gathered0"), sem("gathered1")]
        edge_in = [sem("edge_in0"), sem("edge_in1")]
        edge_done = sem("edge_done")
        added, low_done, t_ready, hot_ready, hotn_ready = (
            sem("added"), sem("low_done"), sem("t_ready"), sem("hot_ready"), sem("hotn_ready"))
        sums_ready, summed = sem("sums_ready"), sem("summed")
        xhot_ready, xhotn_ready, xsums_ready, xsummed = sem("xhot_ready"), sem("xhotn_ready"), sem("xsums_ready"), sem("xsummed")
        count_done, recip_done, hn_done = sem("count_done"), sem("recip_done"), sem("hn_done")
        fin_ps, fin_sum, fin_relu, fin_done, out_done = (
            sem("fin_ps"), sem("fin_sum"), sem("fin_relu"), sem("fin_done"), sem("out_done"))

        block = ctx.enter_context(nc.Block())
        proj_rows = proj.rearrange("(t p) f -> p t f", p=P)
        out_rows = out[0:FULL * P, :].rearrange("(t p) f -> p t f", p=P)
        x_rows = x[0:FULL * P, :].rearrange("(t p) f -> p t f", p=P)

        @block.sync
        def _(sp):
            for c in range(CHUNKS):
                t1 = min((c + 1) * TPC, FULL)
                sp.dma_start(x_sb[:, c * TPC:t1, :], x_rows[:, c * TPC:t1, :]).then_inc(x_in[c], 16)
            sp.wait_ge(rest_zero, 1)
            sp.dma_start(x_sb[0:REST, FULL, :], x[FULL * P:NODES, :]).then_inc(x_in[CHUNKS - 1], 16)
            sp.dma_start(src_sb[:, :], src_cols).then_inc(src_in, 16)
            for s in range(2):
                sp.dma_start(edge_t[:, s, :], edge_rows[s]).then_inc(edge_in[s], 16)
            sp.wait_ge(trips_done, 2)
            sp.dma_start(meta[:, :, :], trips[:, :]).then_inc(meta_in, 16)
            for c in range(CHUNKS):
                sp.wait_ge(proj_sb, c + 1)
                sp.dma_start(proj_rows[:, c * TPC:(c + 1) * TPC, :], p_sb[:, c * TPC:(c + 1) * TPC, :]).then_inc(proj_out, 16)

            def load_edges(g, s):
                sp.wait_ge(edge_done, g - 1)
                sp.dma_start(edge_t[:, s, :], edge_rows[ds(g, 1)].rearrange("a k e -> (a k) e")).then_inc(edge_in[s], 16)

            with sp.Fori(1, (GROUPS - 1) // 2) as i:
                for s in range(2):
                    load_edges(i * 2 + s, s)
            load_edges(GROUPS - 1, 0)
            for c in range(CHUNKS):
                sp.wait_ge(fin_done, c + 1)
                t1 = min((c + 1) * TPC, FULL)
                sp.dma_start(out_rows[:, c * TPC:t1, :], res[:, c * TPC:t1, :]).then_inc(out_done, 16)
            sp.dma_start(out[FULL * P:NODES, :], res[0:REST, FULL, :]).then_inc(out_done, 16)
            sp.wait_ge(out_done, 16 * (CHUNKS + 1))

        @block.gpsimd
        def _(pool):
            nc.gpsimd.memset(x_sb[:, FULL, :], 0.0).then_inc(rest_zero, 1)
            nc.gpsimd.memset(eps[:, :], EPS).then_inc(consts, 1)
            nc.gpsimd.memset(ident[:, :], 0.0).then_inc(consts, 1)
            nc.gpsimd.memset(ones[:, :], 1.0).then_inc(consts, 1)
            pool.wait_ge(consts, 3)
            nc.gpsimd.affine_select(out=ident[:, :], in_=ident[:, :], compare_op=ALU.not_equal, fill=1.0,
                                    base=0, pattern=[[-1, P]], channel_multiplier=1).then_inc(consts, 1)
            nc.gpsimd.memset(w1b_diag[:, :, :], 0.0).then_inc(diag_zero, 1)
            nc.gpsimd.iota(columns[:, :], pattern=[[1, NPAD]], base=0, channel_multiplier=0,
                           allow_small_or_imprecise_dtypes=True).then_inc(consts, 1)
            nc.gpsimd.memset(sums[:, :, :], 0.0).then_inc(consts, 1)
            pool.wait_ge(proj_out, 16 * CHUNKS)

            def gather(s):
                for t in range(TPG):
                    nc.gpsimd.indirect_dma_start(
                        ring[:, s, t, :], None, proj,
                        bass.IndirectOffsetOnAxis(ap=idx[:, s, t:t + 1], axis=0)).then_inc(gathered[s], 16)

            for s in range(2):
                pool.wait_ge(staged, s + 1)
                gather(s)

            def gather_next(g, s):
                pool.wait_ge(added, g - 1)
                pool.sem_inc(pool_tick, 1)
                pool.wait_ge(staged, g + 1)
                pool.sem_inc(pool_tick, 1)
                gather(s)

            with pool.Fori(1, (GROUPS - 1) // 2) as i:
                for s in range(2):
                    gather_next(i * 2 + s, s)
            gather_next(GROUPS - 1, 0)

        @block.scalar
        def _(act):
            def evacuate(c):
                act.wait_ge(turned, c + 1)
                nc.scalar.activation(h_t[:, c * TPC * P:(c + 1) * TPC * P], wide[c % 2], ACT.Relu).then_inc(h_done, 1)
                act.wait_ge(proj_ps, c + 1)
                nc.scalar.copy(p_sb[:, c * TPC:(c + 1) * TPC, :].rearrange("p t f -> p (t f)"), wide[2 + c % 2]).then_inc(proj_sb, 1)

            for dst, source in ((w1a_sb, w1a), (w2a_sb, w2a), (w2b_sb, w2b)):
                act.dma_start(dst[:, :], source).then_inc(w_in, 16)
            act.dma_start(b2_sb[:, :], b2).then_inc(w_in, 16)
            act.dma_start(dst_g[:, :], dst_rows).then_inc(dstg_in, 16)
            act.dma_start(dst_i[:, :], dst_cols).then_inc(dst_in, 16)
            act.wait_ge(diag_zero, 1)
            for t in range(TPG):
                act.dma_start(w1b_diag[t * EDIM:(t + 1) * EDIM, t, :], w1b).then_inc(diag_in, 16)
            act.wait_ge(consts, 6)
            for c in range(CHUNKS):
                tiles = slice(c * TPC, (c + 1) * TPC)
                act.wait_ge(mv_done, c + 1)
                nc.scalar.activation(std[:, tiles], mv[:, tiles, 1], ACT.Sqrt, bias=eps[:, 0:1]).then_inc(std_done, 1)
                if c >= 1:
                    evacuate(c - 1)
            evacuate(CHUNKS - 1)
            for n in range(-(-TILES // 4)):
                k = min(4, TILES - 4 * n)
                act.wait_ge(u_ps, n + 1)
                nc.scalar.copy(u_sb[:, 4 * n:4 * n + k, :], ps[:, 6 + n % 2, 0:k * P].rearrange("p (t f) -> p t f", t=k)).then_inc(u_done, 1)

            def low(g, s):
                act.wait_ge(added, g + 1)
                if not (isinstance(g, int) and g == 0):
                    act.wait_ge(t_ready, g)
                nc.scalar.mul(low_ps, z[:, s].rearrange("p t f -> p (t f)"), SLOPE).then_inc(low_done, 1)

            act.wait_ge(u_done, -(-TILES // 4))
            low(0, 0)
            with act.Fori(0, (GROUPS - 1) // 2) as i:
                low(i * 2 + 1, 1)
                low(i * 2 + 2, 0)
            for c in range(CHUNKS):
                act.wait_ge(fin_sum, c + 1)
                tiles = slice(c * TPC, (c + 1) * TPC)
                nc.scalar.activation(u_sb[:, tiles, :], res[:, tiles, :], ACT.Relu).then_inc(fin_relu, 1)

        @block.vector
        def _(dve):
            def normalize(c):
                tiles = slice(c * TPC, (c + 1) * TPC)
                dve.wait_ge(std_done, c + 1)
                nc.vector.reciprocal(rstd[:, tiles], std[:, tiles]).then_inc(rstd_done, 1)
                dve.wait_ge(rstd_done, c + 1)
                for t in range(c * TPC, (c + 1) * TPC):
                    nc.vector.tensor_scalar(norm[:, t, :], x_sb[:, t, :], mv[:, t, 0:1], rstd[:, t:t + 1],
                                            ALU.subtract, ALU.mult).then_inc(norm_done, 1)

            for c in range(CHUNKS):
                dve.wait_ge(x_in[c], 32 if c == CHUNKS - 1 else 16)
                for t in range(c * TPC, (c + 1) * TPC):
                    nc.vector.bn_stats(stats[:, t, :], x_sb[:, t, :]).then_inc(stats_done, 1)
                dve.wait_ge(stats_done, (c + 1) * TPC)
                for t in range(c * TPC, (c + 1) * TPC):
                    last = nc.vector.bn_aggr(mv[:, t, :], stats[:, t, :])
                last.then_inc(mv_done, 1)
                if c >= 1:
                    normalize(c - 1)
            normalize(CHUNKS - 1)

            dve.wait_ge(dstg_in, 16)
            nc.vector.tensor_reduce(trips[:, 0:1], dst_g[:, :], AX.X, ALU.min).then_inc(span_done, 1)
            nc.vector.tensor_reduce(span[:, 1:2], dst_g[:, :], AX.X, ALU.max).then_inc(span_done, 1)
            dve.wait_ge(span_done, 2)
            nc.vector.tensor_tensor(span[:, 0:1], span[:, 1:2], trips[:, 0:1], ALU.subtract).then_inc(dif_done, 1)
            dve.wait_ge(dif_done, 1)
            nc.vector.tensor_scalar(trips[:, 1:2], span[:, 0:1], SHIFT, None, ALU.logical_shift_right).then_inc(trips_done, 2)
            dve.wait_ge(dst_in, 16)
            nc.vector.tensor_copy(dst_f[:, :], dst_i[:, :]).then_inc(dstf_done, 1)
            dve.wait_ge(src_in, 16)

            def stage(g, s):
                nc.vector.tensor_copy(idx[:, s, :], src_sb[:, ds(g * TPG, TPG)]).then_inc(staged, 1)

            def one_hot(dst, g, at):
                return nc.vector.tensor_tensor(
                    dst, dst_f[:, ds(g * TPG, TPG)].unsqueeze(2).to_broadcast([P, TPG, WIN]),
                    columns[:, ds(at, WIN)].unsqueeze(1).to_broadcast([P, TPG, WIN]), ALU.is_equal)

            def accumulate(source, at):
                part = sums[:, :, ds(at, WIN)]
                return nc.vector.tensor_tensor(part, part, source.rearrange("p (a w) -> p a w", a=2), ALU.add)

            base_reg = dve.alloc_register("base_reg")
            extra_reg = dve.alloc_register("extra_reg")
            at_reg = dve.alloc_register("at_reg")

            stage(0, 0)
            stage(1, 1)
            dve.wait_ge(dstf_done, 1)
            dve.wait_ge(meta_in, 16)
            dve.wait_ge(consts, 6)
            dve.reg_mov(extra_reg, 0)

            def group(g, s, uses, first=False, restage=True):
                base = dve.value_load(meta[0:1, ds(g, 1), 0], min_val=0, max_val=NODES)
                more = dve.value_load(meta[0:1, ds(g, 1), 1], min_val=0, max_val=NODES >> SHIFT)
                dve.wait_ge(edge_done, g + 1)
                dve.wait_ge(gathered[s], uses * 16 * TPG)
                nc.vector.tensor_tensor(z[:, s].rearrange("p t f -> p (t f)"),
                                        ring[:, s].rearrange("p t f -> p (t f)"), msg_ps[s], ALU.add).then_inc(added, 1)
                if restage:
                    stage(g + 2, s)
                dve.wait_ge(sums_ready, g + SLOT_CREDIT - 1)
                one_hot(hot[:, s], g, base).then_inc(hot_ready, 1)
                dve.wait_ge(hot_ready, g + 1)
                nc.vector.tensor_reduce(hot_n[:, s], hot[:, s].rearrange("p t w -> p w t"), AX.X, ALU.add).then_inc(hotn_ready, 1)
                dve.wait_ge(low_done, g + 1)
                nc.vector.tensor_tensor(t_sb[:, s].rearrange("p t f -> p (t f)"),
                                        z[:, s].rearrange("p t f -> p (t f)"), low_ps, ALU.max).then_inc(t_ready, 1)
                if not first:
                    dve.wait_ge(sums_ready, g + SLOT_CREDIT)
                    dve.wait_ge(summed, g + SLOT_CREDIT - 1)
                    accumulate(sum_ps[1 - s], dve.snap(base_reg, min_val=0, max_val=NODES)).then_inc(summed, 1)
                with dve.If(more > 0):
                    dve.reg_mov(at_reg, base)
                    with dve.Fori(0, more):
                        dve.reg_add(at_reg, at_reg, WIN)
                        at = dve.snap(at_reg, min_val=0, max_val=NODES)
                        dve.reg_add(extra_reg, extra_reg, 1)
                        one_hot(hot_x[:, :, :], g, at).then_inc(xhot_ready, 1)
                        extras = dve.snap(extra_reg)
                        dve.wait_ge(xhot_ready, extras)
                        nc.vector.tensor_reduce(hot_xn[:, :], hot_x[:, :, :].rearrange("p t w -> p w t"), AX.X, ALU.add).then_inc(xhotn_ready, 1)
                        dve.wait_ge(summed, g + SLOT_CREDIT)
                        dve.wait_ge(xsums_ready, extras)
                        accumulate(sum_x, at).then_inc(xsummed, 1)
                        dve.wait_ge(xsummed, extras)
                dve.reg_mov(base_reg, base)

            dve.sem_inc(summed, SLOT_CREDIT)
            group(0, 0, 1, first=True)
            with dve.Fori(0, (GROUPS - 3) // 2) as i:
                group(i * 2 + 1, 1, i + 1)
                group(i * 2 + 2, 0, i + 2)
            group(GROUPS - 2, 1, (GROUPS - 1) // 2, restage=False)
            group(GROUPS - 1, 0, (GROUPS + 1) // 2, restage=False)
            dve.wait_ge(sums_ready, GROUPS + SLOT_CREDIT)
            dve.wait_ge(summed, GROUPS - 1 + SLOT_CREDIT)
            accumulate(sum_ps[(GROUPS - 1) % 2], dve.snap(base_reg, min_val=0, max_val=NODES)).then_inc(summed, 1)
            dve.wait_ge(summed, GROUPS + SLOT_CREDIT)
            dve.wait_ge(u_done, -(-TILES // 4))

            for c in range(CHUNKS + 1):
                if c < CHUNKS:
                    cols = slice(c * TPC * P, (c + 1) * TPC * P)
                    if c >= 2:
                        dve.wait_ge(fin_ps, c - 1)
                    nc.vector.tensor_scalar(count[:, c % 2], sums[:, 1, cols], 1.0, None, ALU.max).then_inc(count_done, 1)
                    dve.wait_ge(count_done, c + 1)
                    nc.vector.reciprocal(count[:, c % 2], count[:, c % 2]).then_inc(recip_done, 1)
                    dve.wait_ge(recip_done, c + 1)
                    nc.vector.tensor_tensor(h_n[:, c % 2], sums[:, 0, cols], count[:, c % 2], ALU.mult).then_inc(hn_done, 1)
                if c >= 1:
                    tiles = slice((c - 1) * TPC, c * TPC)
                    dve.wait_ge(fin_ps, c)
                    nc.vector.tensor_tensor(res[:, tiles, :].rearrange("p t f -> p (t f)"),
                                            u_sb[:, tiles, :].rearrange("p t f -> p (t f)"), wide[(c - 1) % 2], ALU.add).then_inc(fin_sum, 1)
                    dve.wait_ge(fin_relu, c)
                    nc.vector.tensor_tensor(res[:, tiles, :], u_sb[:, tiles, :], x_sb[:, tiles, :], ALU.add).then_inc(fin_done, 1)

        @block.tensor
        def _(pe):
            pe.wait_ge(consts, 6)
            pe.wait_ge(w_in, 64)
            for c in range(CHUNKS):
                if c >= 2:
                    pe.wait_ge(h_done, c - 1)
                for j in range(TPC):
                    t = c * TPC + j
                    pe.wait_ge(norm_done, t + 1)
                    last = nc.tensor.transpose(wide[c % 2][:, j * P:(j + 1) * P], norm[:, t, :], ident[:, :])
                last.then_inc(turned, 1)
                pe.wait_ge(h_done, c + 1)
                if c >= 2:
                    pe.wait_ge(proj_sb, c - 1)
                for j in range(TPC):
                    t = c * TPC + j
                    last = nc.tensor.matmul(wide[2 + c % 2][:, j * P:(j + 1) * P], h_t[:, t * P:(t + 1) * P], w1a_sb[:, :],
                                            start=True, stop=True)
                last.then_inc(proj_ps, 1)
            pe.wait_ge(proj_sb, CHUNKS)

            def edge_part(s):
                for half in range(2):
                    last = nc.tensor.matmul(msg_ps[s][:, half * BANK:(half + 1) * BANK], edge_t[:, s, :],
                                            w1b_diag[:, :, :].rearrange("k t f -> k (t f)")[:, half * BANK:(half + 1) * BANK],
                                            start=True, stop=True)
                last.then_inc(edge_done, 1)

            pe.wait_ge(diag_in, 16 * TPG)
            for s in range(2):
                pe.wait_ge(edge_in[s], 16)
                edge_part(s)
            for n in range(-(-TILES // 4)):
                if n >= 2:
                    pe.wait_ge(u_done, n - 1)
                for j in range(min(4, TILES - 4 * n)):
                    t = 4 * n + j
                    dst = ps[:, 6 + n % 2, j * P:(j + 1) * P]
                    nc.tensor.matmul(dst, h_t[:, t * P:(t + 1) * P], w2a_sb[:, :], start=True, stop=False)
                    last = nc.tensor.matmul(dst, ones[0:1, :], b2_sb[:, :], start=False, stop=True)
                last.then_inc(u_ps, 1)
            pe.wait_ge(meta_in, 16)
            pe.sem_inc(sums_ready, SLOT_CREDIT)

            def products(dst, s, one_hots, counts, ready, value):
                for t in range(TPG):
                    nc.tensor.matmul(dst[:, 0:WIN], t_sb[:, s, t, :], one_hots[:, t, :], start=(t == 0), stop=(t == TPG - 1))
                pe.wait_ge(ready, value)
                return nc.tensor.matmul(dst[:, WIN:2 * WIN], ones[:, :], counts, start=True, stop=True)

            extra_reg = pe.alloc_register("pe_extra_reg")
            pe.reg_mov(extra_reg, 0)

            def group(g, s):
                more = pe.value_load(meta[0:1, ds(g, 1), 1], min_val=0, max_val=NODES >> SHIFT)
                pe.wait_ge(summed, g + SLOT_CREDIT - 1)
                pe.wait_ge(hot_ready, g + 1)
                pe.wait_ge(t_ready, g + 1)
                products(sum_ps[s], s, hot[:, s], hot_n[:, s], hotn_ready, g + 1).then_inc(sums_ready, 1)
                with pe.If(more > 0):
                    with pe.Fori(0, more):
                        pe.reg_add(extra_reg, extra_reg, 1)
                        extras = pe.snap(extra_reg)
                        pe.wait_ge(xhot_ready, extras)
                        products(sum_x, s, hot_x[:, :, :], hot_xn[:, :], xhotn_ready, extras).then_inc(xsums_ready, 1)

            def next_edges(g, s, uses):
                pe.wait_ge(added, g - 1)
                pe.wait_ge(edge_in[s], uses * 16)
                edge_part(s)

            with pe.Fori(0, (GROUPS - 3) // 2) as i:
                for s in range(2):
                    group(i * 2 + s, s)
                    next_edges(i * 2 + s + 2, s, i + 2)
            group(GROUPS - 3, 0)
            next_edges(GROUPS - 1, 0, (GROUPS + 1) // 2)
            group(GROUPS - 2, 1)
            group(GROUPS - 1, 0)
            for c in range(CHUNKS):
                pe.wait_ge(hn_done, c + 1)
                if c >= 2:
                    pe.wait_ge(fin_sum, c - 1)
                for j in range(TPC):
                    last = nc.tensor.matmul(wide[c % 2][:, j * P:(j + 1) * P], h_n[:, c % 2, j * P:(j + 1) * P], w2b_sb[:, :],
                                            start=True, stop=True)
                last.then_inc(fin_ps, 1)


def kernel(x, src, dst, edge_attr_3, L0_gnn_W1, L0_gnn_W2, L0_gnn_b2):
    import concourse.bacc as bacc
    from concourse import mybir
    from concourse.bass_utils import run_bass_kernel_spmd

    x, src, dst, edge = (np.asarray(a) for a in (x, src, dst, edge_attr_3))
    w1, w2, b2 = (np.asarray(a) for a in (L0_gnn_W1, L0_gnn_W2, L0_gnn_b2))
    src_pad = np.zeros((LAST_STAGED + 1) * GROUP, src.dtype)
    src_pad[:EDGES] = src
    dst_pad = np.full(GROUPS * GROUP, NODES, dst.dtype)
    dst_pad[:EDGES] = dst
    edge_pad = np.zeros((GROUPS * GROUP, EDIM), edge.dtype)
    edge_pad[:EDGES] = edge
    arrays = {
        "x": x,
        "src_cols": np.ascontiguousarray(src_pad.reshape(-1, P).T),
        "dst_cols": np.ascontiguousarray(dst_pad.reshape(-1, P).T),
        "dst_rows": dst_pad.reshape(GROUPS, GROUP),
        "edge_rows": np.ascontiguousarray(edge_pad.reshape(GROUPS, TPG, P, EDIM).transpose(0, 1, 3, 2).reshape(GROUPS, KE, P)),
        "w1a": np.ascontiguousarray(w1[:, :F].T),
        "w1b": np.ascontiguousarray(w1[:, F:].T),
        "w2a": np.ascontiguousarray(w2[:, :F].T),
        "w2b": np.ascontiguousarray(w2[:, F:].T),
        "b2": b2.reshape(1, F),
    }
    nc = bacc.Bacc("TRN2", target_bir_lowering=False, num_devices=1)
    args = [nc.dram_tensor(k, a.shape, mybir.dt.from_np(a.dtype), kind="ExternalInput").ap() for k, a in arrays.items()]
    proj = nc.dram_tensor("proj", (NPAD, F), mybir.dt.float32, kind="Internal").ap()
    out = nc.dram_tensor("out", (NODES, F), mybir.dt.float32, kind="ExternalOutput").ap()
    build(nc, *args, proj, out)
    result = run_bass_kernel_spmd(nc, [arrays], core_ids=[0])
    return result.results[0]["out"]
```

```python
import numpy as np

P = 128
NODES, EDGES, EDIM = 3125, 103125, 3
F = 128
SLOPE, EPS = 0.01, 1e-5

TPG = 8
GROUP = TPG * P
GROUPS = -(-EDGES // GROUP)
DMA_TILES = TPG - 1
LAST_STAGED = GROUPS + 1
KE = TPG * EDIM

TILES = -(-NODES // P)
FULL = NODES // P
REST = NODES - FULL * P
TPC = 5
CHUNKS = TILES // TPC
NPAD = TILES * P

WIN = 64
SHIFT = 6
assert NPAD >= NODES + 1 + WIN - 1
BANK = 512
SLOT_CREDIT = 2


def build(nc, x, src_cols, src_last, dst_cols, dst_rows, edge_rows, w1a, w1b, w2a, w2b, b2, proj, src_narrow, out):
    import concourse.bass as bass
    from concourse import mybir
    from contextlib import ExitStack

    fp32, bf16, i32, i16 = mybir.dt.float32, mybir.dt.bfloat16, mybir.dt.int32, mybir.dt.int16
    ALU, ACT, AX = mybir.AluOpType, mybir.ActivationFunctionType, mybir.AxisListType
    ds = bass.ds

    with ExitStack() as ctx:
        def sb(name, shape, dt=fp32):
            return ctx.enter_context(nc.sbuf_tensor(name, shape, dt))

        def sem(name):
            return ctx.enter_context(nc.semaphore(name))

        x_sb = sb("x_sb", [P, TILES, F])
        norm = sb("norm", [P, TILES, F])
        h_t = sb("h_t", [F, NPAD])
        p_sb = sb("p_sb", [P, TILES, F])
        u_sb = sb("u_sb", [P, TILES, F])
        stats = sb("stats", [P, TILES, 6])
        mv = sb("mv", [P, TILES, 2])
        std = sb("std", [P, TILES])
        rstd = sb("rstd", [P, TILES])
        eps = sb("eps", [P, 1])
        ident = sb("ident", [P, P])
        ones = sb("ones", [P, P])
        w1a_sb = sb("w1a_sb", [F, F])
        w2a_sb = sb("w2a_sb", [F, F])
        w2b_sb = sb("w2b_sb", [F, F])
        b2_sb = sb("b2_sb", [1, F])
        w1b_diag = sb("w1b_diag", [KE, TPG, F])
        src_sb = sb("src_sb", [P, (LAST_STAGED + 1) * TPG], i32)
        dst_i = sb("dst_i", [P, GROUPS * TPG], i32)
        dst_f = sb("dst_f", [P, GROUPS * TPG])
        dst_g = sb("dst_g", [GROUPS, GROUP], i32)
        span = sb("span", [GROUPS, 2], i32)
        trips = sb("trips", [GROUPS, 2], i32)
        meta = sb("meta", [1, GROUPS, 2], i32)
        columns = sb("columns", [P, NPAD])
        idx = sb("idx", [P, 2, TPG], i32)
        ring = sb("ring", [P, 2, TPG, F])
        edge_t = sb("edge_t", [KE, 2, P])
        t_sb = sb("t_sb", [P, 2, TPG, F])
        t_rest = sb("t_rest", [P, 2, TPG, F])
        t_low = sb("t_low", [P, 2, TPG, F], bf16)
        hot = sb("hot", [P, 2, TPG, WIN], bf16)
        hot_x = sb("hot_x", [P, TPG, WIN], bf16)
        ones_b = sb("ones_b", [P, P], bf16)
        sums = sb("sums", [F, 2, NPAD])
        last_i = sb("last_i", [GROUPS, P], i32)
        last_n = sb("last_n", [GROUPS, P], i16)
        src_all = sb("src_all", [P, 2, P], i16)
        node_of = sb("node_of", [P, TILES, P], i16)
        hot_t = sb("hot_t", [P, 2, TILES, P], bf16)
        p_parts = sb("p_parts", [P, TILES, 3, F], bf16)
        degree = sb("degree", [P, TILES])
        inv_degree = sb("inv_degree", [P, TILES])
        res = norm
        p_rest = norm

        def upper(a):
            return a.bitcast(bf16).rearrange("p (f h) -> p f h", h=2)[:, :, 1]

        ps = ctx.enter_context(nc.psum_tensor("ps", [P, 8, BANK], fp32))
        flat = ps[:, :, :].rearrange("p b c -> p (b c)")
        edge_ps = flat[:, 0:DMA_TILES * F]
        last_ps = [ps[:, 2, 0:F], ps[:, 3, 0:F]]
        sum_ps = [flat[:, 4 * BANK:4 * BANK + 2 * WIN], flat[:, 5 * BANK:5 * BANK + 2 * WIN]]
        sum_x = flat[:, 4 * BANK + 2 * P:4 * BANK + 2 * P + 2 * WIN]
        low_ps = flat[:, 6 * BANK:8 * BANK]
        wide = [flat[:, 2 * b * BANK:2 * b * BANK + TPC * P] for b in range(4)]

        x_in = [sem(f"x_in{c}") for c in range(CHUNKS)]
        rest_zero = sem("rest_zero")
        consts = sem("consts")
        diag_zero = sem("diag_zero")
        w_in = sem("w_in")
        diag_in = sem("diag_in")
        src_in, dst_in, dstg_in = sem("src_in"), sem("dst_in"), sem("dstg_in")
        stats_done, mv_done, std_done, rstd_done = sem("stats_done"), sem("mv_done"), sem("std_done"), sem("rstd_done")
        norm_done, turned, h_done = sem("norm_done"), sem("turned"), sem("h_done")
        proj_ps, proj_sb, proj_out = sem("proj_ps"), sem("proj_sb"), sem("proj_out")
        u_ps, u_done = sem("u_ps"), sem("u_done")
        span_done, dif_done, trips_done, meta_in, dstf_done = (
            sem("span_done"), sem("dif_done"), sem("trips_done"), sem("meta_in"), sem("dstf_done"))
        narrow_in, narrowed, narrow_out = sem("narrow_in"), sem("narrowed"), sem("narrow_out")
        parts0, rest1, parts1, parts2 = sem("parts0"), sem("rest1"), sem("parts1"), sem("parts2")
        staged = sem("staged")
        pool_tick = sem("pool_tick")
        gathered = [sem("gathered0"), sem("gathered1")]
        edge_in = [sem("edge_in0"), sem("edge_in1")]
        src_all_in = [sem("src_all_in0"), sem("src_all_in1")]
        edge_done, filled, picked, last_filled, hott_ready = (
            sem("edge_done"), sem("filled"), sem("picked"), sem("last_filled"), sem("hott_ready"))
        low_done, t_ready, rest_ready, parts_ready, hot_ready = (
            sem("low_done"), sem("t_ready"), sem("rest_ready"), sem("parts_ready"), sem("hot_ready"))
        sums_ready, summed = sem("sums_ready"), sem("summed")
        xhot_ready, xsums_ready, xsummed = sem("xhot_ready"), sem("xsums_ready"), sem("xsummed")
        degree_ps, degree_done, inv_done = sem("degree_ps"), sem("degree_done"), sem("inv_done")
        fin_ps, fin_sum, fin_done, out_done = sem("fin_ps"), sem("fin_sum"), sem("fin_done"), sem("out_done")

        block = ctx.enter_context(nc.Block())
        proj_rows = proj.rearrange("(t p) f -> p t f", p=P)
        out_rows = out[0:FULL * P, :].rearrange("(t p) f -> p t f", p=P)
        x_rows = x[0:FULL * P, :].rearrange("(t p) f -> p t f", p=P)

        @block.sync
        def _(sp):
            for c in range(CHUNKS):
                t1 = min((c + 1) * TPC, FULL)
                sp.dma_start(x_sb[:, c * TPC:t1, :], x_rows[:, c * TPC:t1, :]).then_inc(x_in[c], 16)
            sp.wait_ge(rest_zero, 1)
            sp.dma_start(x_sb[0:REST, FULL, :], x[FULL * P:NODES, :]).then_inc(x_in[CHUNKS - 1], 16)
            sp.dma_start(src_sb[:, :], src_cols).then_inc(src_in, 16)
            for s in range(2):
                sp.dma_start(edge_t[:, s, :], edge_rows[s]).then_inc(edge_in[s], 16)
            sp.dma_start(last_i[:, :], src_last).then_inc(narrow_in, 16)
            sp.wait_ge(trips_done, 2)
            sp.dma_start(meta[:, :, :], trips[:, :]).then_inc(meta_in, 16)
            for c in range(CHUNKS):
                sp.wait_ge(proj_sb, c + 1)
                sp.dma_start(proj_rows[:, c * TPC:(c + 1) * TPC, :], p_sb[:, c * TPC:(c + 1) * TPC, :]).then_inc(proj_out, 16)
            sp.wait_ge(narrowed, 1)
            sp.dma_start(src_narrow, last_n[:, :]).then_inc(narrow_out, 16)
            sp.wait_ge(narrow_out, 16)

            def load_sources(g, s):
                sp.dma_start(src_all[:, s, :], src_narrow[ds(g, 1), :].to_broadcast([P, P])).then_inc(src_all_in[s], 16)

            load_sources(0, 0)
            load_sources(1, 1)

            def load_group(g, s):
                sp.wait_ge(edge_done, g - 1)
                sp.dma_start(edge_t[:, s, :], edge_rows[ds(g, 1)].rearrange("a k e -> (a k) e")).then_inc(edge_in[s], 16)
                sp.wait_ge(hott_ready, g - 1)
                load_sources(g, s)

            with sp.Fori(1, (GROUPS - 1) // 2) as i:
                for s in range(2):
                    load_group(i * 2 + s, s)
            load_group(GROUPS - 1, 0)
            for c in range(CHUNKS):
                sp.wait_ge(fin_done, c + 1)
                t1 = min((c + 1) * TPC, FULL)
                sp.dma_start(out_rows[:, c * TPC:t1, :], res[:, c * TPC:t1, :]).then_inc(out_done, 16)
            sp.dma_start(out[FULL * P:NODES, :], res[0:REST, FULL, :]).then_inc(out_done, 16)
            sp.wait_ge(out_done, 16 * (CHUNKS + 1))

        @block.gpsimd
        def _(pool):
            nc.gpsimd.memset(x_sb[:, FULL, :], 0.0).then_inc(rest_zero, 1)
            nc.gpsimd.memset(eps[:, :], EPS).then_inc(consts, 1)
            nc.gpsimd.memset(ident[:, :], 0.0).then_inc(consts, 1)
            nc.gpsimd.memset(ones[:, :], 1.0).then_inc(consts, 1)
            pool.wait_ge(consts, 3)
            nc.gpsimd.affine_select(out=ident[:, :], in_=ident[:, :], compare_op=ALU.not_equal, fill=1.0,
                                    base=0, pattern=[[-1, P]], channel_multiplier=1).then_inc(consts, 1)
            nc.gpsimd.memset(w1b_diag[:, :, :], 0.0).then_inc(diag_zero, 1)
            nc.gpsimd.iota(columns[:, :], pattern=[[1, NPAD]], base=0, channel_multiplier=0,
                           allow_small_or_imprecise_dtypes=True).then_inc(consts, 1)
            nc.gpsimd.iota(node_of[:, :, :], pattern=[[P, TILES], [0, P]], base=0, channel_multiplier=1,
                           allow_small_or_imprecise_dtypes=True).then_inc(consts, 1)
            nc.gpsimd.memset(ones_b[:, :], 1.0).then_inc(consts, 1)
            nc.gpsimd.memset(sums[:, :, :], 0.0).then_inc(consts, 1)
            pool.wait_ge(proj_out, 16 * CHUNKS)

            def gather(g, s):
                pool.wait_ge(staged, g + 1)
                pool.sem_inc(pool_tick, 1)
                pool.wait_ge(filled, g + 1)
                pool.sem_inc(pool_tick, 1)
                for t in range(DMA_TILES):
                    nc.gpsimd.indirect_dma_start(
                        ring[:, s, t, :], None, proj,
                        bass.IndirectOffsetOnAxis(ap=idx[:, s, t:t + 1], axis=0),
                        compute_op=ALU.add).then_inc(gathered[s], 16)

            gather(0, 0)
            gather(1, 1)
            with pool.Fori(1, (GROUPS - 1) // 2) as i:
                for s in range(2):
                    gather(i * 2 + s, s)
            gather(GROUPS - 1, 0)

        @block.scalar
        def _(act):
            def evacuate(c):
                act.wait_ge(turned, c + 1)
                nc.scalar.activation(h_t[:, c * TPC * P:(c + 1) * TPC * P], wide[c % 2], ACT.Relu).then_inc(h_done, 1)
                act.wait_ge(proj_ps, c + 1)
                nc.scalar.copy(p_sb[:, c * TPC:(c + 1) * TPC, :].rearrange("p t f -> p (t f)"), wide[2 + c % 2]).then_inc(proj_sb, 1)

            for dst, source in ((w1a_sb, w1a), (w2a_sb, w2a), (w2b_sb, w2b)):
                act.dma_start(dst[:, :], source).then_inc(w_in, 16)
            act.dma_start(b2_sb[:, :], b2).then_inc(w_in, 16)
            act.dma_start(dst_g[:, :], dst_rows).then_inc(dstg_in, 16)
            act.dma_start(dst_i[:, :], dst_cols).then_inc(dst_in, 16)
            act.wait_ge(diag_zero, 1)
            for t in range(TPG):
                act.dma_start(w1b_diag[t * EDIM:(t + 1) * EDIM, t, :], w1b).then_inc(diag_in, 16)
            act.wait_ge(consts, 8)
            for c in range(CHUNKS):
                tiles = slice(c * TPC, (c + 1) * TPC)
                act.wait_ge(mv_done, c + 1)
                nc.scalar.activation(std[:, tiles], mv[:, tiles, 1], ACT.Sqrt, bias=eps[:, 0:1]).then_inc(std_done, 1)
                if c >= 1:
                    evacuate(c - 1)
            evacuate(CHUNKS - 1)

            def split_parts(which, source, done):
                nc.scalar.copy(p_parts[:, :, which, :], source[:, :, :]).then_inc(done, 1)

            def fill(g, s):
                act.wait_ge(edge_done, g + 1)
                nc.scalar.copy(ring[:, s, 0:DMA_TILES, :].rearrange("p t f -> p (t f)"),
                               edge_ps).then_inc(filled, 1)

            def fill_last(g, s):
                act.wait_ge(picked, g + 1)
                nc.scalar.copy(ring[:, s, DMA_TILES, :], last_ps[s]).then_inc(last_filled, 1)

            def low(g, s, uses):
                act.wait_ge(last_filled, g + 1)
                act.wait_ge(gathered[s], uses * 16 * DMA_TILES)
                if not (isinstance(g, int) and g == 0):
                    act.wait_ge(t_ready, g)
                nc.scalar.mul(low_ps, ring[:, s].rearrange("p t f -> p (t f)"), SLOPE).then_inc(low_done, 1)

            def refill(g, s):
                act.wait_ge(t_ready, g - 1)
                fill(g, s)
                fill_last(g, s)

            fill(0, 0)
            fill(1, 1)
            act.wait_ge(proj_sb, CHUNKS)
            split_parts(0, p_sb, parts0)
            act.wait_ge(rest1, 1)
            split_parts(1, p_rest, parts1)
            for n in range(-(-TILES // 4)):
                k = min(4, TILES - 4 * n)
                act.wait_ge(u_ps, n + 1)
                nc.scalar.copy(u_sb[:, 4 * n:4 * n + k, :], ps[:, 6 + n % 2, 0:k * P].rearrange("p (t f) -> p t f", t=k)).then_inc(u_done, 1)
            fill_last(0, 0)
            fill_last(1, 1)
            act.wait_ge(u_done, -(-TILES // 4))
            low(0, 0, 1)
            refill(2, 0)
            with act.Fori(0, (GROUPS - 3) // 2) as i:
                low(i * 2 + 1, 1, i + 1)
                refill(i * 2 + 3, 1)
                low(i * 2 + 2, 0, i + 2)
                refill(i * 2 + 4, 0)
            low(GROUPS - 2, 1, (GROUPS - 1) // 2)
            low(GROUPS - 1, 0, (GROUPS + 1) // 2)

        @block.vector
        def _(dve):
            def normalize(c):
                tiles = slice(c * TPC, (c + 1) * TPC)
                dve.wait_ge(std_done, c + 1)
                nc.vector.reciprocal(rstd[:, tiles], std[:, tiles]).then_inc(rstd_done, 1)
                dve.wait_ge(rstd_done, c + 1)
                for t in range(c * TPC, (c + 1) * TPC):
                    nc.vector.tensor_scalar(norm[:, t, :], x_sb[:, t, :], mv[:, t, 0:1], rstd[:, t:t + 1],
                                            ALU.subtract, ALU.mult).then_inc(norm_done, 1)

            for c in range(CHUNKS):
                dve.wait_ge(x_in[c], 32 if c == CHUNKS - 1 else 16)
                for t in range(c * TPC, (c + 1) * TPC):
                    nc.vector.bn_stats(stats[:, t, :], x_sb[:, t, :]).then_inc(stats_done, 1)
                dve.wait_ge(stats_done, (c + 1) * TPC)
                for t in range(c * TPC, (c + 1) * TPC):
                    last = nc.vector.bn_aggr(mv[:, t, :], stats[:, t, :])
                last.then_inc(mv_done, 1)
                if c >= 1:
                    normalize(c - 1)
            normalize(CHUNKS - 1)

            dve.wait_ge(dstg_in, 16)
            nc.vector.tensor_reduce(trips[:, 0:1], dst_g[:, :], AX.X, ALU.min).then_inc(span_done, 1)
            nc.vector.tensor_reduce(span[:, 1:2], dst_g[:, :], AX.X, ALU.max).then_inc(span_done, 1)
            dve.wait_ge(span_done, 2)
            nc.vector.tensor_tensor(span[:, 0:1], span[:, 1:2], trips[:, 0:1], ALU.subtract).then_inc(dif_done, 1)
            dve.wait_ge(dif_done, 1)
            nc.vector.tensor_scalar(trips[:, 1:2], span[:, 0:1], SHIFT, None, ALU.logical_shift_right).then_inc(trips_done, 2)
            dve.wait_ge(dst_in, 16)
            nc.vector.tensor_copy(dst_f[:, :], dst_i[:, :]).then_inc(dstf_done, 1)
            dve.wait_ge(narrow_in, 16)
            nc.vector.tensor_copy(last_n[:, :], last_i[:, :]).then_inc(narrowed, 1)
            dve.wait_ge(src_in, 16)

            def stage(g, s):
                nc.vector.tensor_copy(idx[:, s, :], src_sb[:, ds(g * TPG, TPG)]).then_inc(staged, 1)

            def one_hot(dst, g, at):
                return nc.vector.tensor_tensor(
                    dst, dst_f[:, ds(g * TPG, TPG)].unsqueeze(2).to_broadcast([P, TPG, WIN]),
                    columns[:, ds(at, WIN)].unsqueeze(1).to_broadcast([P, TPG, WIN]), ALU.is_equal)

            def accumulate(source, at):
                part = sums[:, :, ds(at, WIN)]
                return nc.vector.tensor_tensor(part, part, source.rearrange("p (a w) -> p a w", a=2), ALU.add)

            def one_hot_sources(g, s, uses):
                dve.wait_ge(src_all_in[s], uses * 16)
                nc.vector.tensor_tensor(hot_t[:, s], src_all[:, s, :].unsqueeze(1).to_broadcast([P, TILES, P]),
                                        node_of[:, :, :], ALU.is_equal).then_inc(hott_ready, 1)

            prev_reg = dve.alloc_register("prev_reg")
            base_reg = dve.alloc_register("base_reg")
            extra_reg = dve.alloc_register("extra_reg")
            at_reg = dve.alloc_register("at_reg")

            stage(0, 0)
            stage(1, 1)
            dve.wait_ge(parts0, 1)
            dve.wait_ge(turned, CHUNKS)
            nc.vector.tensor_tensor(p_rest[:, :, :], p_sb[:, :, :], p_parts[:, :, 0, :], ALU.subtract).then_inc(rest1, 1)
            dve.wait_ge(parts1, 1)
            nc.vector.tensor_tensor(p_parts[:, :, 2, :], p_rest[:, :, :], p_parts[:, :, 1, :], ALU.subtract).then_inc(parts2, 1)
            dve.wait_ge(dstf_done, 1)
            dve.wait_ge(meta_in, 16)
            dve.wait_ge(consts, 8)
            dve.sem_inc(summed, SLOT_CREDIT)
            for g in range(2):
                one_hot_sources(g, g, 1)
            first = dve.value_load(meta[0:1, 0:1, 0], min_val=0, max_val=NODES)
            one_hot(hot[:, 0], 0, first).then_inc(hot_ready, 1)
            dve.reg_mov(base_reg, first)
            dve.reg_mov(extra_reg, 0)
            dve.wait_ge(picked, 1)
            one_hot_sources(2, 0, 2)

            def group(g, s, uses, first=False, restage=True, sources=True, last=False):
                base = dve.snap(base_reg, min_val=0, max_val=NODES)
                more = dve.value_load(meta[0:1, ds(g, 1), 1], min_val=0, max_val=NODES >> SHIFT)
                msgs, low = ring[:, s].rearrange("p t f -> p (t f)"), low_ps
                whole, rest, least = (a[:, s].rearrange("p t f -> p (t f)") for a in (t_sb, t_rest, t_low))
                dve.wait_ge(sums_ready, g + SLOT_CREDIT - 1)
                dve.wait_ge(low_done, g + 1)
                nc.vector.tensor_tensor(whole, msgs, low, ALU.max).then_inc(t_ready, 1)
                if restage:
                    stage(g + 2, s)
                dve.wait_ge(t_ready, g + 1)
                nc.vector.tensor_tensor(rest, whole, upper(whole), ALU.subtract).then_inc(rest_ready, 1)
                dve.wait_ge(rest_ready, g + 1)
                nc.vector.tensor_tensor(least, rest, upper(rest), ALU.subtract).then_inc(parts_ready, 1)
                if not first:
                    dve.wait_ge(sums_ready, g + SLOT_CREDIT)
                    dve.wait_ge(summed, g + SLOT_CREDIT - 1)
                    accumulate(sum_ps[1 - s], dve.snap(prev_reg, min_val=0, max_val=NODES)).then_inc(summed, 1)
                with dve.If(more > 0):
                    dve.reg_mov(at_reg, base)
                    with dve.Fori(0, more):
                        dve.reg_add(at_reg, at_reg, WIN)
                        at = dve.snap(at_reg, min_val=0, max_val=NODES)
                        dve.reg_add(extra_reg, extra_reg, 1)
                        extras = dve.snap(extra_reg)
                        one_hot(hot_x[:, :, :], g, at).then_inc(xhot_ready, 1)
                        dve.wait_ge(summed, g + SLOT_CREDIT)
                        dve.wait_ge(xsums_ready, extras)
                        accumulate(sum_x, at).then_inc(xsummed, 1)
                        dve.wait_ge(xsummed, extras)
                dve.reg_mov(prev_reg, base)
                if not last:
                    following = dve.value_load(meta[0:1, ds(g + 1, 1), 0], min_val=0, max_val=NODES)
                    if first:
                        one_hot(hot[:, 1 - s], g + 1, following).then_inc(hot_ready, 1)
                    else:
                        dve.wait_ge(sums_ready, g + SLOT_CREDIT)
                        one_hot(hot[:, 1 - s], g + 1, following).then_inc(hot_ready, 1)
                    dve.reg_mov(base_reg, following)
                if sources:
                    dve.wait_ge(picked, g + 2)
                    one_hot_sources(g + 3, 1 - s, uses)

            group(0, 0, 2, first=True)
            with dve.Fori(0, (GROUPS - 5) // 2) as i:
                group(i * 2 + 1, 1, i + 3)
                group(i * 2 + 2, 0, i + 3)
            group(GROUPS - 4, 1, (GROUPS + 1) // 2)
            group(GROUPS - 3, 0, 0, sources=False)
            group(GROUPS - 2, 1, 0, restage=False, sources=False)
            group(GROUPS - 1, 0, 0, restage=False, sources=False, last=True)
            dve.wait_ge(sums_ready, GROUPS + SLOT_CREDIT)
            dve.wait_ge(summed, GROUPS - 1 + SLOT_CREDIT)
            accumulate(sum_ps[(GROUPS - 1) % 2], dve.snap(base_reg, min_val=0, max_val=NODES)).then_inc(summed, 1)

            dve.wait_ge(degree_ps, 1)
            nc.vector.tensor_scalar(degree[:, :], low_ps[:, 0:TILES], 1.0, None, ALU.max).then_inc(degree_done, 1)
            dve.wait_ge(degree_done, 1)
            nc.vector.reciprocal(inv_degree[:, :], degree[:, :]).then_inc(inv_done, 1)
            dve.wait_ge(inv_done, 1)
            for c in range(CHUNKS):
                tiles = slice(c * TPC, (c + 1) * TPC)
                dve.wait_ge(fin_ps, c + 1)
                for j in range(TPC):
                    t = c * TPC + j
                    part = wide[c % 3][:, j * P:(j + 1) * P]
                    nc.vector.scalar_tensor_tensor(part, part, inv_degree[:, t:t + 1], u_sb[:, t, :], ALU.mult, ALU.add).then_inc(fin_sum, 1)
                dve.wait_ge(fin_sum, (c + 1) * TPC)
                nc.vector.scalar_tensor_tensor(res[:, tiles, :].rearrange("p t f -> p (t f)"), wide[c % 3], 0.0,
                                               x_sb[:, tiles, :].rearrange("p t f -> p (t f)"), ALU.max, ALU.add).then_inc(fin_done, 1)

        @block.tensor
        def _(pe):
            pe.wait_ge(consts, 8)
            pe.wait_ge(w_in, 64)
            for c in range(CHUNKS):
                if c >= 2:
                    pe.wait_ge(h_done, c - 1)
                for j in range(TPC):
                    t = c * TPC + j
                    pe.wait_ge(norm_done, t + 1)
                    last = nc.tensor.transpose(wide[c % 2][:, j * P:(j + 1) * P], norm[:, t, :], ident[:, :])
                last.then_inc(turned, 1)
                pe.wait_ge(h_done, c + 1)
                if c >= 2:
                    pe.wait_ge(proj_sb, c - 1)
                for j in range(TPC):
                    t = c * TPC + j
                    last = nc.tensor.matmul(wide[2 + c % 2][:, j * P:(j + 1) * P], h_t[:, t * P:(t + 1) * P], w1a_sb[:, :],
                                            start=True, stop=True)
                last.then_inc(proj_ps, 1)
            pe.wait_ge(proj_sb, CHUNKS)

            def edge_part(s):
                diag = w1b_diag[:, :, :].rearrange("k t f -> k (t f)")
                nc.tensor.matmul(last_ps[s], edge_t[:, s, :], diag[:, DMA_TILES * F:TPG * F], start=True, stop=False)
                for lo, hi in ((0, BANK), (BANK, DMA_TILES * F)):
                    last = nc.tensor.matmul(edge_ps[:, lo:hi], edge_t[:, s, :], diag[:, lo:hi], start=True, stop=True)
                last.then_inc(edge_done, 1)

            def pick(s):
                for c in range(TILES):
                    for part in range(3):
                        last = nc.tensor.matmul(last_ps[s], hot_t[:, s, c, :], p_parts[:, c, part, :],
                                                start=False, stop=(c == TILES - 1 and part == 2))
                last.then_inc(picked, 1)

            pe.wait_ge(diag_in, 16 * TPG)
            for s in range(2):
                pe.wait_ge(edge_in[s], 16)
                if s == 1:
                    pe.wait_ge(filled, 1)
                edge_part(s)
            for n in range(-(-TILES // 4)):
                if n >= 2:
                    pe.wait_ge(u_done, n - 1)
                for j in range(min(4, TILES - 4 * n)):
                    t = 4 * n + j
                    dst = ps[:, 6 + n % 2, j * P:(j + 1) * P]
                    nc.tensor.matmul(dst, h_t[:, t * P:(t + 1) * P], w2a_sb[:, :], start=True, stop=False)
                    last = nc.tensor.matmul(dst, ones[0:1, :], b2_sb[:, :], start=False, stop=True)
                last.then_inc(u_ps, 1)
            pe.wait_ge(parts2, 1)
            for s in range(2):
                pe.wait_ge(hott_ready, s + 1)
                pick(s)
            pe.wait_ge(meta_in, 16)
            pe.sem_inc(sums_ready, SLOT_CREDIT)

            def products(dst, s, one_hots):
                for t in range(TPG):
                    parts = (upper(t_sb[:, s, t, :]), upper(t_rest[:, s, t, :]), t_low[:, s, t, :])
                    for n, part in enumerate(parts):
                        nc.tensor.matmul(dst[:, 0:WIN], part, one_hots[:, t, :],
                                         start=(t == 0 and n == 0), stop=(t == TPG - 1 and n == 2))
                for t in range(TPG):
                    last = nc.tensor.matmul(dst[:, WIN:2 * WIN], ones_b[:, :], one_hots[:, t, :],
                                            start=(t == 0), stop=(t == TPG - 1))
                return last

            extra_reg = pe.alloc_register("pe_extra_reg")
            pe.reg_mov(extra_reg, 0)

            def group(g, s):
                more = pe.value_load(meta[0:1, ds(g, 1), 1], min_val=0, max_val=NODES >> SHIFT)
                pe.wait_ge(summed, g + SLOT_CREDIT - 1)
                pe.wait_ge(hot_ready, g + 1)
                pe.wait_ge(parts_ready, g + 1)
                products(sum_ps[s], s, hot[:, s]).then_inc(sums_ready, 1)
                with pe.If(more > 0):
                    with pe.Fori(0, more):
                        pe.reg_add(extra_reg, extra_reg, 1)
                        extras = pe.snap(extra_reg)
                        pe.wait_ge(xhot_ready, extras)
                        products(sum_x, s, hot_x[:, :, :]).then_inc(xsums_ready, 1)

            def next_rows(g, s, uses):
                pe.wait_ge(filled, g)
                pe.wait_ge(last_filled, g - 1)
                pe.wait_ge(edge_in[s], uses * 16)
                edge_part(s)
                pe.wait_ge(hott_ready, g + 1)
                pick(s)

            with pe.Fori(0, (GROUPS - 3) // 2) as i:
                for s in range(2):
                    next_rows(i * 2 + s + 2, s, i + 2)
                    group(i * 2 + s, s)
            next_rows(GROUPS - 1, 0, (GROUPS + 1) // 2)
            group(GROUPS - 3, 0)
            group(GROUPS - 2, 1)
            group(GROUPS - 1, 0)
            pe.wait_ge(summed, GROUPS + SLOT_CREDIT)
            for t in range(TILES):
                last = nc.tensor.matmul(low_ps[:, t:t + 1], sums[0:1, 1, t * P:(t + 1) * P], ones[0:1, 0:1], start=True, stop=True)
            last.then_inc(degree_ps, 1)
            for c in range(CHUNKS):
                if c >= 3:
                    pe.wait_ge(fin_done, c - 2)
                for j in range(TPC):
                    t = c * TPC + j
                    last = nc.tensor.matmul(wide[c % 3][:, j * P:(j + 1) * P], sums[:, 0, t * P:(t + 1) * P], w2b_sb[:, :],
                                            start=True, stop=True)
                last.then_inc(fin_ps, 1)


def kernel(x, src, dst, edge_attr_3, L0_gnn_W1, L0_gnn_W2, L0_gnn_b2):
    import concourse.bacc as bacc
    from concourse import mybir
    from concourse.bass_utils import run_bass_kernel_spmd

    x, src, dst, edge = (np.asarray(a) for a in (x, src, dst, edge_attr_3))
    w1, w2, b2 = (np.asarray(a) for a in (L0_gnn_W1, L0_gnn_W2, L0_gnn_b2))
    src_pad = np.zeros((LAST_STAGED + 1) * GROUP, src.dtype)
    src_pad[:EDGES] = src
    dst_pad = np.full(GROUPS * GROUP, NODES, dst.dtype)
    dst_pad[:EDGES] = dst
    edge_pad = np.zeros((GROUPS * GROUP, EDIM), edge.dtype)
    edge_pad[:EDGES] = edge
    arrays = {
        "x": x,
        "src_cols": np.ascontiguousarray(src_pad.reshape(-1, P).T),
        "src_last": np.ascontiguousarray(src_pad[:GROUPS * GROUP].reshape(GROUPS, TPG, P)[:, TPG - 1]),
        "dst_cols": np.ascontiguousarray(dst_pad.reshape(-1, P).T),
        "dst_rows": dst_pad.reshape(GROUPS, GROUP),
        "edge_rows": np.ascontiguousarray(edge_pad.reshape(GROUPS, TPG, P, EDIM).transpose(0, 1, 3, 2).reshape(GROUPS, KE, P)),
        "w1a": np.ascontiguousarray(w1[:, :F].T),
        "w1b": np.ascontiguousarray(w1[:, F:].T),
        "w2a": np.ascontiguousarray(w2[:, :F].T),
        "w2b": np.ascontiguousarray(w2[:, F:].T),
        "b2": b2.reshape(1, F),
    }
    nc = bacc.Bacc("TRN2", target_bir_lowering=False, num_devices=1)
    args = [nc.dram_tensor(k, a.shape, mybir.dt.from_np(a.dtype), kind="ExternalInput").ap() for k, a in arrays.items()]
    proj = nc.dram_tensor("proj", (NPAD, F), mybir.dt.float32, kind="Internal").ap()
    src_narrow = nc.dram_tensor("src_narrow", (GROUPS, P), mybir.dt.int16, kind="Internal").ap()
    out = nc.dram_tensor("out", (NODES, F), mybir.dt.float32, kind="ExternalOutput").ap()
    build(nc, *args, proj, src_narrow, out)
    result = run_bass_kernel_spmd(nc, [arrays], core_ids=[0])
    return result.results[0]["out"]
```

```python
import numpy as np

P = 128
NODES, EDGES, EDIM = 3125, 103125, 3
F = 128
SLOPE, EPS = 0.01, 1e-5

TPG = 7
GROUP = TPG * P
GROUPS = -(-EDGES // GROUP)
DMA_TILES = TPG - 1
LAST_TILES = -(-(EDGES - (GROUPS - 1) * GROUP) // P)
assert LAST_TILES < TPG
LAST_STAGED = GROUPS + 1
KE = TPG * EDIM
PAIRS = ((0, 0), (0, 1), (0, 2), (1, 0), (1, 1), (2, 0))
KS = len(PAIRS) * KE
assert KS <= P
LOOPED = 2 * ((GROUPS - 5) // 2)
LATE, LAST = GROUPS - 2, GROUPS - 1

TILES = -(-NODES // P)
FULL = NODES // P
REST = NODES - FULL * P
TPC = 5
CHUNKS = TILES // TPC
NPAD = TILES * P

WIN = 64
SHIFT = 6
assert NPAD >= NODES + 1 + WIN - 1
BANK = 512
SLOT_CREDIT = 2


def build(nc, x, src_cols, src_last, dst_cols, dst_rows, edge_rows, split_signs, w1a, w1b_rows, w2a, w2b, b2, proj, src_narrow, out):
    import concourse.bass as bass
    from concourse import mybir
    from contextlib import ExitStack

    fp32, bf16, i32, i16 = mybir.dt.float32, mybir.dt.bfloat16, mybir.dt.int32, mybir.dt.int16
    ALU, ACT, AX = mybir.AluOpType, mybir.ActivationFunctionType, mybir.AxisListType
    ds = bass.ds

    with ExitStack() as ctx:
        def sb(name, shape, dt=fp32):
            return ctx.enter_context(nc.sbuf_tensor(name, shape, dt))

        def sem(name):
            return ctx.enter_context(nc.semaphore(name))

        x_sb = sb("x_sb", [P, TILES, F])
        norm = sb("norm", [P, TILES, F])
        h_t = sb("h_t", [F, NPAD])
        p_sb = sb("p_sb", [P, TILES, F])
        u_sb = sb("u_sb", [P, TILES, F])
        stats = sb("stats", [P, TILES, 6])
        mv = sb("mv", [P, TILES, 2])
        std = sb("std", [P, TILES])
        rstd = sb("rstd", [P, TILES])
        eps = sb("eps", [P, 1])
        ident = sb("ident", [P, P])
        w1a_sb = sb("w1a_sb", [F, F])
        w2a_sb = sb("w2a_sb", [F, F])
        w2b_sb = sb("w2b_sb", [F, F])
        b2_all = sb("b2_all", [P, F])
        w_raw = sb("w_raw", [KS, TPG * F])
        w_rest = sb("w_rest", [KS, TPG * F])
        w_split = sb("w_split", [KS, TPG * F])
        signs = sb("signs", [KS, 4])
        src_sb = sb("src_sb", [P, (LAST_STAGED + 1) * TPG], i32)
        dst_i = sb("dst_i", [P, GROUPS * TPG], i32)
        dst_n = sb("dst_n", [P, GROUPS * TPG], i16)
        dst_g = sb("dst_g", [GROUPS, GROUP], i32)
        span = sb("span", [GROUPS, 2], i32)
        trips = sb("trips", [GROUPS, 2], i32)
        meta = sb("meta", [1, GROUPS, 2], i32)
        columns = sb("columns", [P, NPAD], i16)
        idx = sb("idx", [P, 2, TPG], i32)
        ring = sb("ring", [P, 2, TPG, F])
        e_raw = sb("e_raw", [KS, 2, P])
        e_rest = sb("e_rest", [KS, 2, P])
        e_split = sb("e_split", [KS, 2, P])
        t_sb = sb("t_sb", [P, 2, TPG, F])
        t_rest = sb("t_rest", [P, 2, TPG, F])
        t_low = sb("t_low", [P, 2, TPG, F], bf16)
        hot = sb("hot", [P, 2, TPG, WIN], bf16)
        hot_x = sb("hot_x", [P, TPG, WIN], bf16)
        ones_b = sb("ones_b", [P, P], bf16)
        sums = sb("sums", [F, 2, NPAD])
        last_i = sb("last_i", [GROUPS, P], i32)
        last_n = sb("last_n", [GROUPS, P], i16)
        src_all = sb("src_all", [P, 2, P], i16)
        node_of = sb("node_of", [P, TILES, P], i16)
        hot_t = sb("hot_t", [P, 2, TILES, P], bf16)
        p_parts = sb("p_parts", [P, TILES, 3, F], bf16)
        degree = sb("degree", [P, TILES])
        inv_degree = sb("inv_degree", [P, TILES])
        p_rest = norm
        res = norm

        def upper(a):
            return a.bitcast(bf16).rearrange("p (f h) -> p f h", h=2)[:, :, 1]

        ps = ctx.enter_context(nc.psum_tensor("ps", [P, 8, BANK], fp32))
        flat = ps[:, :, :].rearrange("p b c -> p (b c)")
        edge_ps = flat[:, 0:DMA_TILES * F]
        last_ps = [ps[:, 2, 0:F], ps[:, 3, 0:F]]
        sum_ps = [flat[:, 4 * BANK:4 * BANK + 2 * WIN], flat[:, 5 * BANK:5 * BANK + 2 * WIN]]
        sum_x = flat[:, 4 * BANK + 2 * P:4 * BANK + 2 * P + 2 * WIN]
        late_x = [flat[:, b * BANK + 3 * P:b * BANK + 3 * P + WIN] for b in (4, 5)]
        low_ps = flat[:, 6 * BANK:6 * BANK + TPG * F]
        count_ps = [ps[:, n, 0:WIN] for n in range(2)]
        count_x = [ps[:, n, WIN:2 * WIN] for n in range(2)]
        degree_cols = ps[:, 1, 4 * WIN:4 * WIN + TILES]
        wide = [flat[:, 2 * b * BANK:2 * b * BANK + TPC * P] for b in range(4)]

        x_in = [sem(f"x_in{c}") for c in range(CHUNKS)]
        rest_zero = sem("rest_zero")
        early, consts = sem("early"), sem("consts")
        w1_in, w2_in, b2_in = sem("w1_in"), sem("w2_in"), sem("b2_in")
        signs_in, w1b_in = sem("signs_in"), sem("w1b_in")
        w_resting, w_ready = sem("w_resting"), sem("w_ready")
        e_resting, split_ready = sem("e_resting"), sem("split_ready")
        src_in, dst_in, dstg_in = sem("src_in"), sem("dst_in"), sem("dstg_in")
        stats_done, mv_done, std_done, rstd_done = sem("stats_done"), sem("mv_done"), sem("std_done"), sem("rstd_done")
        norm_done, turned, h_done = sem("norm_done"), sem("turned"), sem("h_done")
        proj_ps, proj_sb, proj_out = sem("proj_ps"), sem("proj_sb"), sem("proj_out")
        u_ps, u_done, u_biased = sem("u_ps"), sem("u_done"), sem("u_biased")
        span_done, dif_done, trips_done, meta_in, dstf_done = (
            sem("span_done"), sem("dif_done"), sem("trips_done"), sem("meta_in"), sem("dstf_done"))
        narrow_in, narrowed, narrow_out = sem("narrow_in"), sem("narrowed"), sem("narrow_out")
        parts0, parts1, parts2 = sem("parts0"), sem("parts1"), sem("parts2")
        staged = sem("staged")
        pool_tick = sem("pool_tick")
        gathered = [sem("gathered0"), sem("gathered1")]
        edge_in = [sem("edge_in0"), sem("edge_in1")]
        src_all_in = [sem("src_all_in0"), sem("src_all_in1")]
        edge_done, filled, picked, last_filled, hott_ready = (
            sem("edge_done"), sem("filled"), sem("picked"), sem("last_filled"), sem("hott_ready"))
        low_done, t_ready, rest_ready, parts_ready, hot_ready = (
            sem("low_done"), sem("t_ready"), sem("rest_ready"), sem("parts_ready"), sem("hot_ready"))
        sums_ready, summed = sem("sums_ready"), sem("summed")
        counts_ready, counted, all_counted = sem("counts_ready"), sem("counted"), sem("all_counted")
        xhot_ready, xsums_ready, xsummed = sem("xhot_ready"), sem("xsums_ready"), sem("xsummed")
        degree_ps, degree_done, inv_done = sem("degree_ps"), sem("degree_done"), sem("inv_done")
        fin_ps, fin_mean, fin_sum, fin_relu, out_done = sem("fin_ps"), sem("fin_mean"), sem("fin_sum"), sem("fin_relu"), sem("out_done")

        U_STEPS = -(-TILES // 4)
        U_BEFORE = 2
        U_EARLY = 2
        U_MIDDLE = 3

        OUT_TILES = BANK // F
        OUT_STEPS = -(-TILES // OUT_TILES)

        assert OUT_STEPS == 7

        def out_tiles(n):
            return n * OUT_TILES, min((n + 1) * OUT_TILES, TILES)

        def out_ps(n):
            lo, hi = out_tiles(n)
            return ps[:, n, 0:(hi - lo) * F].rearrange("p (t f) -> p t f", f=F)

        def on_pool(n):
            return n in (0, 2)

        POOL_RESTS = 4
        rest1 = [sem(f"rest1_{c}") for c in range(CHUNKS)]

        def take_first_part(engine, c):
            tiles = slice(c * TPC, (c + 1) * TPC)
            engine.tensor_tensor(p_rest[:, tiles, :], p_sb[:, tiles, :], p_parts[:, tiles, 0, :], ALU.subtract).then_inc(rest1[c], 1)

        fin_done = [sem(f"fin_done{n}") for n in range(OUT_STEPS)]
        block = ctx.enter_context(nc.Block())
        proj_rows = proj.rearrange("(t p) f -> p t f", p=P)
        out_rows = out[0:FULL * P, :].rearrange("(t p) f -> p t f", p=P)
        x_rows = x[0:FULL * P, :].rearrange("(t p) f -> p t f", p=P)

        @block.sync
        def _(sp):
            for c in range(CHUNKS):
                t1 = min((c + 1) * TPC, FULL)
                sp.dma_start(x_sb[:, c * TPC:t1, :], x_rows[:, c * TPC:t1, :]).then_inc(x_in[c], 16)
            sp.wait_ge(rest_zero, 1)
            sp.dma_start(x_sb[0:REST, FULL, :], x[FULL * P:NODES, :]).then_inc(x_in[CHUNKS - 1], 16)
            sp.dma_start(last_i[:, :], src_last).then_inc(narrow_in, 16)
            sp.dma_start(signs[:, :], split_signs).then_inc(signs_in, 16)
            sp.dma_start(w_raw[:, :], w1b_rows).then_inc(w1b_in, 16)
            sp.dma_start(src_sb[:, :], src_cols).then_inc(src_in, 16)
            for s in range(2):
                sp.dma_start(e_raw[:, s, :], edge_rows[s]).then_inc(edge_in[s], 16)
            sp.dma_start(dst_g[:, :], dst_rows).then_inc(dstg_in, 16)
            sp.dma_start(dst_i[:, :], dst_cols).then_inc(dst_in, 16)
            sp.wait_ge(narrowed, 1)
            sp.dma_start(src_narrow, last_n[:, :]).then_inc(narrow_out, 16)
            sp.wait_ge(narrow_out, 16)

            def load_sources(g, s):
                sp.dma_start(src_all[:, s, :], src_narrow[ds(g, 1), :].to_broadcast([P, P])).then_inc(src_all_in[s], 16)

            load_sources(0, 0)
            load_sources(1, 1)
            for c in range(CHUNKS):
                sp.wait_ge(proj_sb, c + 1)
                sp.dma_start(proj_rows[:, c * TPC:(c + 1) * TPC, :], p_sb[:, c * TPC:(c + 1) * TPC, :]).then_inc(proj_out, 16)

            def load_edges(g, s):
                sp.wait_ge(split_ready, g - 1)
                sp.dma_start(e_raw[:, s, :], edge_rows[ds(g, 1)].rearrange("a k e -> (a k) e")).then_inc(edge_in[s], 16)

            def next_sources(g, s):
                sp.wait_ge(hott_ready, g - 1)
                load_sources(g, s)

            for g in (2, 3):
                load_edges(g, g % 2)
            next_sources(2, 0)
            load_edges(4, 0)
            next_sources(3, 1)
            with sp.Fori(1, LOOPED // 2 + 1) as i:
                for s in (1, 0):
                    load_edges(i * 2 + 4 - s, s)
                    next_sources(i * 2 + 3 - s, 1 - s)
            for g in range(LOOPED + 1, LATE - 2):
                load_edges(g + 4, g % 2)
                next_sources(g + 3, (g + 1) % 2)
            for n in (1, 0, 3, 4, 2, 5, 6):
                sp.wait_ge(fin_done[n], 1)
                lo, hi = out_tiles(n)
                if lo < FULL:
                    sp.dma_start(out_rows[:, lo:min(hi, FULL), :], res[:, lo:min(hi, FULL), :]).then_inc(out_done, 16)
            sp.dma_start(out[FULL * P:NODES, :], res[0:REST, FULL, :]).then_inc(out_done, 16)
            sp.wait_ge(out_done, 16 * (-(-FULL // OUT_TILES) + 1))

        @block.gpsimd
        def _(pool):
            nc.gpsimd.memset(x_sb[:, FULL, :], 0.0).then_inc(rest_zero, 1)
            nc.gpsimd.memset(eps[:, :], EPS).then_inc(early, 1)
            nc.gpsimd.memset(ident[:, :], 0.0).then_inc(early, 1)
            pool.wait_ge(early, 2)
            nc.gpsimd.affine_select(out=ident[:, :], in_=ident[:, :], compare_op=ALU.not_equal, fill=1.0,
                                    base=0, pattern=[[-1, P]], channel_multiplier=1).then_inc(early, 1)
            nc.gpsimd.iota(node_of[:, :, :], pattern=[[P, TILES], [0, P]], base=0, channel_multiplier=1,
                           allow_small_or_imprecise_dtypes=True).then_inc(consts, 1)
            nc.gpsimd.iota(columns[:, :], pattern=[[1, NPAD]], base=0, channel_multiplier=0,
                           allow_small_or_imprecise_dtypes=True).then_inc(consts, 1)
            nc.gpsimd.memset(ones_b[:, :], 1.0).then_inc(consts, 1)
            nc.gpsimd.memset(sums[:, :, :], 0.0).then_inc(consts, 1)
            for c in range(POOL_RESTS):
                pool.wait_ge(turned, c + 1)
                pool.wait_ge(proj_sb, c + 1)
                pool.wait_ge(parts0, c + 1)
                take_first_part(nc.gpsimd, c)
            pool.wait_ge(proj_out, 16 * CHUNKS)

            def gather(g, s, tiles=DMA_TILES):
                pool.wait_ge(staged, g + 1)
                pool.sem_inc(pool_tick, 1)
                pool.wait_ge(filled, g + 1)
                pool.sem_inc(pool_tick, 1)
                for t in range(tiles):
                    nc.gpsimd.indirect_dma_start(
                        ring[:, s, t, :], None, proj,
                        bass.IndirectOffsetOnAxis(ap=idx[:, s, t:t + 1], axis=0),
                        compute_op=ALU.add).then_inc(gathered[s], 16)

            gather(0, 0)
            gather(1, 1)
            with pool.Fori(1, LOOPED // 2) as i:
                for s in range(2):
                    gather(i * 2 + s, s)
            for g in range(LOOPED, LAST):
                gather(g, g % 2)
            gather(LAST, LAST % 2, LAST_TILES)
            pool.wait_ge(b2_in, 16)
            for n in range(OUT_STEPS):
                lo, hi = out_tiles(n)
                pool.wait_ge(u_done, n + 1)
                nc.gpsimd.tensor_tensor(u_sb[:, lo:hi, :], u_sb[:, lo:hi, :],
                                        b2_all[:, :].unsqueeze(1).to_broadcast([P, hi - lo, F]), ALU.add).then_inc(u_biased, 1)
            for n in range(OUT_STEPS):
                if on_pool(n):
                    tiles = slice(*out_tiles(n))
                    pool.wait_ge(fin_sum, n + 1)
                    nc.gpsimd.tensor_scalar(res[:, tiles, :], u_sb[:, tiles, :], 0.0, None, ALU.max).then_inc(fin_relu, 1)
                    pool.wait_ge(fin_relu, n // 2 + 1)
                    nc.gpsimd.tensor_tensor(res[:, tiles, :], res[:, tiles, :], x_sb[:, tiles, :], ALU.add).then_inc(fin_done[n], 1)

        @block.scalar
        def _(act):
            def inverse_std(c):
                tiles = slice(c * TPC, (c + 1) * TPC)
                act.wait_ge(mv_done, c + 1)
                nc.scalar.activation(std[:, tiles], mv[:, tiles, 1], ACT.Sqrt, bias=eps[:, 0:1]).then_inc(std_done, 1)

            act.dma_start(w1a_sb[:, :], w1a).then_inc(w1_in, 16)
            act.wait_ge(early, 3)
            inverse_std(0)
            act.dma_start(w2a_sb[:, :], w2a).then_inc(w2_in, 16)
            act.dma_start(w2b_sb[:, :], w2b).then_inc(w2_in, 16)
            act.dma_start(b2_all[:, :], b2.to_broadcast([P, F])).then_inc(b2_in, 16)
            inverse_std(1)

            def transposed_relu(c):
                act.wait_ge(turned, c + 1)
                nc.scalar.activation(h_t[:, c * TPC * P:(c + 1) * TPC * P], wide[c % 2], ACT.Relu).then_inc(h_done, 1)

            def second_part(c):
                tiles = slice(c * TPC, (c + 1) * TPC)
                act.wait_ge(rest1[c], 1)
                nc.scalar.copy(p_parts[:, tiles, 1, :], p_rest[:, tiles, :]).then_inc(parts1, 1)

            transposed_relu(0)
            inverse_std(2)
            for c in range(CHUNKS):
                if c + 1 < CHUNKS:
                    transposed_relu(c + 1)
                if c + 3 < CHUNKS:
                    inverse_std(c + 3)
                tiles = slice(c * TPC, (c + 1) * TPC)
                projected = wide[2 + c % 2].rearrange("p (t f) -> p t f", f=F)
                act.wait_ge(proj_ps, c + 1)
                nc.scalar.copy(p_sb[:, tiles, :], projected).then_inc(proj_sb, 1)
                nc.scalar.copy(p_parts[:, tiles, 0, :], projected).then_inc(parts0, 1)

            def keep_u(n):
                k = min(4, TILES - 4 * n)
                act.wait_ge(u_ps, n + 1)
                nc.scalar.copy(u_sb[:, 4 * n:4 * n + k, :], ps[:, 2 + n % 2, 0:k * P].rearrange("p (t f) -> p t f", t=k)).then_inc(u_done, 1)

            def fill(g, s):
                act.wait_ge(edge_done, g + 1)
                nc.scalar.copy(ring[:, s, 0:DMA_TILES, :].rearrange("p t f -> p (t f)"), edge_ps).then_inc(filled, 1)

            def fill_last(g, s):
                act.wait_ge(picked, g + 1)
                nc.scalar.copy(ring[:, s, DMA_TILES, :], last_ps[s]).then_inc(last_filled, 1)

            def low(g, s, uses):
                act.wait_ge(last_filled, g + 1)
                act.wait_ge(gathered[s], uses * 16 * DMA_TILES)
                if not (isinstance(g, int) and g == 0):
                    act.wait_ge(t_ready, g)
                nc.scalar.mul(low_ps, ring[:, s].rearrange("p t f -> p (t f)"), SLOPE).then_inc(low_done, 1)

            def last_low(g, s, uses):
                act.wait_ge(gathered[s], (uses - 1) * 16 * DMA_TILES + 16 * LAST_TILES)
                act.wait_ge(t_ready, g)
                nc.scalar.mul(low_ps[:, 0:LAST_TILES * F], ring[:, s, 0:LAST_TILES].rearrange("p t f -> p (t f)"),
                              SLOPE).then_inc(low_done, 1)

            def refill(g, s):
                act.wait_ge(t_ready, g - 1)
                fill(g, s)

            fill(0, 0)
            for c in range(CHUNKS):
                second_part(c)
            fill(1, 1)
            fill_last(0, 0)
            act.wait_ge(parts0, CHUNKS)
            low(0, 0, 1)
            act.wait_ge(trips_done, 2)
            act.dma_start(meta[:, :, :], trips[:, :]).then_inc(meta_in, 16)
            refill(2, 0)
            fill_last(1, 1)
            with act.Fori(0, LOOPED // 2) as i:
                low(i * 2 + 1, 1, i + 1)
                refill(i * 2 + 3, 1)
                fill_last(i * 2 + 2, 0)
                low(i * 2 + 2, 0, i + 2)
                refill(i * 2 + 4, 0)
                fill_last(i * 2 + 3, 1)
            for g in range(LOOPED + 1, LATE):
                low(g, g % 2, g // 2 + 1)
                if g + 1 == LATE:
                    fill_last(g + 1, (g + 1) % 2)
                refill(g + 2, g % 2)
                if g + 1 < LATE:
                    fill_last(g + 1, (g + 1) % 2)
            for n in range(U_BEFORE):
                keep_u(n)
            low(LATE, LATE % 2, LATE // 2 + 1)
            for n in range(U_BEFORE, U_STEPS):
                keep_u(n)
            last_low(LAST, LAST % 2, LAST // 2 + 1)
            act.wait_ge(inv_done, 1)
            for n in range(OUT_STEPS):
                act.wait_ge(fin_ps, n + 1)
                for t in range(*out_tiles(n)):
                    part = out_ps(n)[:, t % OUT_TILES, :]
                    nc.scalar.mul(part, part, inv_degree[:, t:t + 1]).then_inc(fin_mean, 1)

        @block.vector
        def _(dve):
            def normalize(c):
                tiles = slice(c * TPC, (c + 1) * TPC)
                dve.wait_ge(std_done, c + 1)
                nc.vector.reciprocal(rstd[:, tiles], std[:, tiles]).then_inc(rstd_done, 1)
                dve.wait_ge(rstd_done, c + 1)
                for t in range(c * TPC, (c + 1) * TPC):
                    nc.vector.tensor_scalar(norm[:, t, :], x_sb[:, t, :], mv[:, t, 0:1], rstd[:, t:t + 1],
                                            ALU.subtract, ALU.mult).then_inc(norm_done, 1)

            for c in range(CHUNKS):
                dve.wait_ge(x_in[c], 32 if c == CHUNKS - 1 else 16)
                for t in range(c * TPC, (c + 1) * TPC):
                    nc.vector.bn_stats(stats[:, t, :], x_sb[:, t, :]).then_inc(stats_done, 1)
                dve.wait_ge(stats_done, (c + 1) * TPC)
                for t in range(c * TPC, (c + 1) * TPC):
                    last = nc.vector.bn_aggr(mv[:, t, :], stats[:, t, :])
                last.then_inc(mv_done, 1)
                if c >= 1:
                    normalize(c - 1)
                if c == 1:
                    dve.wait_ge(narrow_in, 16)
                    nc.vector.tensor_copy(last_n[:, :], last_i[:, :]).then_inc(narrowed, 1)
            normalize(CHUNKS - 1)

            def stage(g, s):
                nc.vector.tensor_copy(idx[:, s, :], src_sb[:, ds(g * TPG, TPG)]).then_inc(staged, 1)

            def split_w(step):
                before, after, done = ((w_raw, w_rest, w_resting), (w_rest, w_split, w_ready))[step]
                if step > 0:
                    dve.wait_ge(w_resting, 1)
                nc.vector.scalar_tensor_tensor(after[:, :], upper(before[:, :]), signs[:, 2 + step:3 + step], before[:, :],
                                               ALU.mult, ALU.add).then_inc(done, 1)

            def split_edges(g, s, uses, step):
                if step == 0:
                    dve.wait_ge(edge_in[s], uses * 16)
                    before, after, done = e_raw, e_rest, e_resting
                else:
                    dve.wait_ge(e_resting, g + 1)
                    before, after, done = e_rest, e_split, split_ready
                nc.vector.scalar_tensor_tensor(after[:, s, :], upper(before[:, s, :]), signs[:, step:step + 1], before[:, s, :],
                                               ALU.mult, ALU.add).then_inc(done, 1)

            dve.wait_ge(signs_in, 16)
            dve.wait_ge(w1b_in, 16)
            split_w(0)
            split_edges(0, 0, 1, 0)
            split_w(1)
            split_edges(0, 0, 1, 1)
            dve.wait_ge(src_in, 16)
            stage(0, 0)
            stage(1, 1)

            def rest_part(c):
                dve.wait_ge(turned, c + 1)
                dve.wait_ge(proj_sb, c + 1)
                dve.wait_ge(parts0, c + 1)
                take_first_part(nc.vector, c)

            def third_part(c):
                tiles = slice(c * TPC, (c + 1) * TPC)
                dve.wait_ge(parts1, c + 1)
                nc.vector.tensor_tensor(p_parts[:, tiles, 2, :], p_rest[:, tiles, :], p_parts[:, tiles, 1, :], ALU.subtract).then_inc(parts2, 1)

            def one_hot_sources(g, s, uses):
                dve.wait_ge(src_all_in[s], uses * 16)
                nc.vector.tensor_tensor(hot_t[:, s], src_all[:, s, :].unsqueeze(1).to_broadcast([P, TILES, P]),
                                        node_of[:, :, :], ALU.is_equal).then_inc(hott_ready, 1)

            dve.wait_ge(consts, 1)
            one_hot_sources(0, 0, 1)
            for c in range(POOL_RESTS, CHUNKS):
                rest_part(c)
            split_edges(1, 1, 1, 0)
            third_part(0)
            split_edges(1, 1, 1, 1)
            for c in range(1, CHUNKS):
                third_part(c)
            one_hot_sources(1, 1, 1)
            for g in (2, 3):
                dve.wait_ge(edge_done, g - 1)
                for step in range(2):
                    split_edges(g, g % 2, 2, step)

            dve.wait_ge(dstg_in, 16)
            nc.vector.tensor_reduce(trips[:, 0:1], dst_g[:, :], AX.X, ALU.min).then_inc(span_done, 1)
            nc.vector.tensor_reduce(span[:, 1:2], dst_g[:, :], AX.X, ALU.max).then_inc(span_done, 1)
            dve.wait_ge(span_done, 2)
            nc.vector.tensor_tensor(span[:, 0:1], span[:, 1:2], trips[:, 0:1], ALU.subtract).then_inc(dif_done, 1)
            dve.wait_ge(dif_done, 1)
            nc.vector.tensor_scalar(trips[:, 1:2], span[:, 0:1], SHIFT, None, ALU.logical_shift_right).then_inc(trips_done, 2)
            dve.wait_ge(dst_in, 16)
            nc.vector.tensor_copy(dst_n[:, :], dst_i[:, :]).then_inc(dstf_done, 1)
            def one_hot(dst, g, at):
                return nc.vector.tensor_tensor(
                    dst, dst_n[:, ds(g * TPG, TPG)].unsqueeze(2).to_broadcast([P, TPG, WIN]),
                    columns[:, ds(at, WIN)].unsqueeze(1).to_broadcast([P, TPG, WIN]), ALU.is_equal)

            def accumulate(source, at):
                part = sums[:, :, ds(at, WIN)]
                return nc.vector.tensor_tensor(part, part, source.rearrange("p (a w) -> p a w", a=2), ALU.add)

            def add_row(row, source, at):
                part = sums[:, row, ds(at, WIN)]
                return nc.vector.tensor_tensor(part, part, source, ALU.add)

            prev_reg = dve.alloc_register("prev_reg")
            base_reg = dve.alloc_register("base_reg")
            extra_reg = dve.alloc_register("extra_reg")
            at_reg = dve.alloc_register("at_reg")

            def leaky_parts(low_count, s, lo=0, hi=TPG, between=lambda step: None):
                msgs, whole, rest, least = (
                    a[:, s, lo:hi].rearrange("p t f -> p (t f)") for a in (ring, t_sb, t_rest, t_low))
                dve.wait_ge(low_done, low_count)
                nc.vector.tensor_tensor(whole, msgs, low_ps[:, lo * F:hi * F], ALU.max).then_inc(t_ready, 1)
                between(0)
                dve.wait_ge(t_ready, low_count)
                nc.vector.tensor_tensor(rest, whole, upper(whole), ALU.subtract).then_inc(rest_ready, 1)
                between(1)
                dve.wait_ge(rest_ready, low_count)
                nc.vector.tensor_tensor(least, rest, upper(rest), ALU.subtract).then_inc(parts_ready, 1)

            def windows_beyond(g):
                return dve.value_load(meta[0:1, ds(g, 1), 1], min_val=0, max_val=NODES >> SHIFT)

            def extra_windows(g, base, more, added, add):
                with dve.If(more > 0):
                    dve.reg_mov(at_reg, base)
                    with dve.Fori(0, more):
                        dve.reg_add(at_reg, at_reg, WIN)
                        at = dve.snap(at_reg, min_val=0, max_val=NODES)
                        dve.reg_add(extra_reg, extra_reg, 1)
                        extras = dve.snap(extra_reg)
                        one_hot(hot_x[:, :, :], g, at).then_inc(xhot_ready, 1)
                        dve.wait_ge(summed, added)
                        dve.wait_ge(xsums_ready, extras)
                        add(at).then_inc(xsummed, 1)
                        dve.wait_ge(xsummed, extras)

            def least_node(g):
                return dve.value_load(meta[0:1, ds(g, 1), 0], min_val=0, max_val=NODES)

            def prepare_next(g, s, uses, sources=True):
                following = least_node(g + 1)
                one_hot(hot[:, 1 - s], g + 1, following).then_inc(hot_ready, 1)
                dve.reg_mov(base_reg, following)
                if sources:
                    dve.wait_ge(picked, g + 2)
                    one_hot_sources(g + 3, 1 - s, uses)

            def group(g, s, uses, full=True):
                base = dve.snap(base_reg, min_val=0, max_val=NODES)
                more = windows_beyond(g)
                dve.wait_ge(sums_ready, g + SLOT_CREDIT - 1)

                def between(step):
                    if step == 0:
                        stage(g + 2, s)
                        if full:
                            dve.wait_ge(edge_done, g + 3)
                    if full:
                        split_edges(g + 4, s, uses[1], step)

                leaky_parts(g + 1, s, between=between)
                dve.wait_ge(sums_ready, g + SLOT_CREDIT)
                dve.wait_ge(summed, g + SLOT_CREDIT - 1)
                accumulate(sum_ps[1 - s], dve.snap(prev_reg, min_val=0, max_val=NODES)).then_inc(summed, 1)
                extra_windows(g, base, more, g + SLOT_CREDIT, lambda at: accumulate(sum_x, at))
                dve.reg_mov(prev_reg, base)
                prepare_next(g, s, uses[0], full)

            def before_parts(step):
                if step == 0:
                    stage(2, 0)
                    dve.wait_ge(picked, 1)
                    one_hot_sources(2, 0, 2)
                    dve.wait_ge(edge_done, 3)
                split_edges(4, 0, 3, step)

            leaky_parts(1, 0, between=before_parts)
            dve.wait_ge(dstf_done, 1)
            dve.wait_ge(meta_in, 16)
            dve.wait_ge(consts, 4)
            dve.sem_inc(summed, SLOT_CREDIT)
            base = least_node(0)
            one_hot(hot[:, 0], 0, base).then_inc(hot_ready, 1)
            dve.reg_mov(extra_reg, 0)
            extra_windows(0, base, windows_beyond(0), SLOT_CREDIT, lambda at: accumulate(sum_x, at))
            dve.reg_mov(prev_reg, base)
            prepare_next(0, 0, 2)
            with dve.Fori(0, LOOPED // 2) as i:
                group(i * 2 + 1, 1, (i + 3, i + 3))
                group(i * 2 + 2, 0, (i + 3, i + 4))
            for g in range(LOOPED + 1, LATE):
                group(g, g % 2, ((g + 3) // 2 + 1, (g + 4) // 2 + 1), full=g + 4 < GROUPS)
            ends = {g: (least_node(g), windows_beyond(g)) for g in (LATE, LAST)}
            dve.wait_ge(sums_ready, LATE + SLOT_CREDIT)
            dve.wait_ge(summed, LATE - 1 + SLOT_CREDIT)
            accumulate(sum_ps[LAST % 2], dve.snap(prev_reg, min_val=0, max_val=NODES)).then_inc(summed, 1)
            one_hot(hot[:, LAST % 2], LAST, ends[LAST][0]).then_inc(hot_ready, 1)
            dve.wait_ge(summed, LATE + SLOT_CREDIT)
            for n, g in enumerate((LATE, LAST)):
                dve.wait_ge(counts_ready, n + 1)
                if n > 0:
                    dve.wait_ge(counted, n)
                add_row(1, count_ps[n], ends[g][0]).then_inc(counted, 1)
                dve.wait_ge(counted, n + 1)
                extra_windows(g, *ends[g], LATE + SLOT_CREDIT, lambda at: add_row(1, count_x[n], at))
            dve.sem_inc(all_counted, 1)
            leaky_parts(LATE + 1, LATE % 2)
            leaky_parts(LAST + 1, LAST % 2, 0, LAST_TILES)
            dve.wait_ge(degree_ps, 1)
            nc.vector.tensor_scalar(degree[:, :], degree_cols, 1.0, None, ALU.max).then_inc(degree_done, 1)
            dve.wait_ge(degree_done, 1)
            nc.vector.reciprocal(inv_degree[:, :], degree[:, :]).then_inc(inv_done, 1)
            for g in (LATE, LAST):
                extra_windows(g, *ends[g], g + SLOT_CREDIT, lambda at: add_row(0, late_x[g % 2], at))
                dve.wait_ge(sums_ready, g + 1 + SLOT_CREDIT)
                dve.wait_ge(summed, g + SLOT_CREDIT)
                add_row(0, sum_ps[g % 2][:, 0:WIN], ends[g][0]).then_inc(summed, 1)

            for n in range(OUT_STEPS + 1):
                if n > 0 and not on_pool(n - 1):
                    tiles = slice(*out_tiles(n - 1))
                    dve.wait_ge(fin_sum, n)
                    nc.vector.scalar_tensor_tensor(res[:, tiles, :], u_sb[:, tiles, :], 0.0, x_sb[:, tiles, :],
                                                   ALU.max, ALU.add).then_inc(fin_done[n - 1], 1)
                if n < OUT_STEPS:
                    whole = u_sb[:, slice(*out_tiles(n)), :]
                    dve.wait_ge(fin_mean, min((n + 1) * OUT_TILES, TILES))
                    dve.wait_ge(u_biased, n + 1)
                    nc.vector.tensor_tensor(whole, out_ps(n), whole, ALU.add).then_inc(fin_sum, 1)

        @block.tensor
        def _(pe):
            def turn(c):
                if c >= 2:
                    pe.wait_ge(h_done, c - 1)
                for j in range(TPC):
                    t = c * TPC + j
                    pe.wait_ge(norm_done, t + 1)
                    last = nc.tensor.transpose(wide[c % 2][:, j * P:(j + 1) * P], norm[:, t, :], ident[:, :])
                last.then_inc(turned, 1)

            pe.wait_ge(early, 3)
            turn(0)
            pe.wait_ge(w1_in, 16)
            for c in range(CHUNKS):
                if c + 1 < CHUNKS:
                    turn(c + 1)
                pe.wait_ge(h_done, c + 1)
                if c >= 2:
                    pe.wait_ge(proj_sb, c - 1)
                    pe.wait_ge(parts0, c - 1)
                for j in range(TPC):
                    t = c * TPC + j
                    last = nc.tensor.matmul(wide[2 + c % 2][:, j * P:(j + 1) * P], h_t[:, t * P:(t + 1) * P], w1a_sb[:, :],
                                            start=True, stop=True)
                last.then_inc(proj_ps, 1)

            def edge_part(s, whole=True):
                attributes, diag = upper(e_split[:, s, :]), upper(w_split[:, :])
                if whole:
                    nc.tensor.matmul(last_ps[s], attributes, diag[:, DMA_TILES * F:TPG * F], start=True, stop=False)
                for lo, hi in ((0, BANK), (BANK, DMA_TILES * F)):
                    last = nc.tensor.matmul(edge_ps[:, lo:hi], attributes, diag[:, lo:hi], start=True, stop=True)
                last.then_inc(edge_done, 1)

            def pick(s, arriving=False):
                for part in range(3):
                    if arriving:
                        pe.wait_ge((parts0, parts1, parts2)[part], CHUNKS)
                    for c in range(TILES):
                        last = nc.tensor.matmul(last_ps[s], hot_t[:, s, c, :], p_parts[:, c, part, :],
                                                start=False, stop=(c == TILES - 1 and part == 2))
                last.then_inc(picked, 1)

            def own_part(n):
                if n >= 2:
                    pe.wait_ge(u_done, n - 1)
                for j in range(min(4, TILES - 4 * n)):
                    t = 4 * n + j
                    last = nc.tensor.matmul(ps[:, 2 + n % 2, j * P:(j + 1) * P], h_t[:, t * P:(t + 1) * P], w2a_sb[:, :],
                                            start=True, stop=True)
                last.then_inc(u_ps, 1)

            pe.wait_ge(w_ready, 1)
            pe.wait_ge(split_ready, 1)
            edge_part(0)
            pe.wait_ge(split_ready, 2)
            pe.wait_ge(filled, 1)
            edge_part(1)
            pe.sem_inc(sums_ready, SLOT_CREDIT)
            pe.wait_ge(hott_ready, 1)
            pick(0, arriving=True)
            pe.wait_ge(filled, 2)
            pe.wait_ge(last_filled, 1)
            pe.wait_ge(split_ready, 3)
            edge_part(0)
            pe.wait_ge(hott_ready, 2)
            pick(1)
            pe.wait_ge(meta_in, 16)
            pe.wait_ge(parts0, CHUNKS)
            pe.wait_ge(consts, 3)

            def message_sums(dst, s, one_hots, tiles=TPG):
                for t in range(tiles):
                    parts = (upper(t_sb[:, s, t, :]), upper(t_rest[:, s, t, :]), t_low[:, s, t, :])
                    for n, part in enumerate(parts):
                        last = nc.tensor.matmul(dst[:, 0:WIN], part, one_hots[:, t, :],
                                                start=(t == 0 and n == 0), stop=(t == tiles - 1 and n == 2))
                return last

            def edge_counts(dst, one_hots, tiles=TPG):
                for t in range(tiles):
                    last = nc.tensor.matmul(dst, ones_b[:, :], one_hots[:, t, :], start=(t == 0), stop=(t == tiles - 1))
                return last

            def both(dst, s, one_hots):
                message_sums(dst, s, one_hots)
                return edge_counts(dst[:, WIN:2 * WIN], one_hots)

            extra_reg = pe.alloc_register("pe_extra_reg")
            pe.reg_mov(extra_reg, 0)

            def windows_beyond(g):
                return pe.value_load(meta[0:1, ds(g, 1), 1], min_val=0, max_val=NODES >> SHIFT)

            def extra_windows(more, products):
                with pe.If(more > 0):
                    with pe.Fori(0, more):
                        pe.reg_add(extra_reg, extra_reg, 1)
                        extras = pe.snap(extra_reg)
                        pe.wait_ge(xhot_ready, extras)
                        products().then_inc(xsums_ready, 1)

            def group(g, s):
                more = windows_beyond(g)
                pe.wait_ge(summed, g + SLOT_CREDIT - 1)
                pe.wait_ge(hot_ready, g + 1)
                pe.wait_ge(parts_ready, g + 1)
                both(sum_ps[s], s, hot[:, s]).then_inc(sums_ready, 1)
                extra_windows(more, lambda: both(sum_x, s, hot_x))

            def next_edges(g, s, whole=True):
                pe.wait_ge(filled, g)
                if whole:
                    pe.wait_ge(last_filled, g - 1)
                pe.wait_ge(split_ready, g + 1)
                edge_part(s, whole)

            def next_pick(g, s):
                pe.wait_ge(hott_ready, g + 1)
                pick(s)

            next_edges(3, 1)
            next_pick(2, 0)
            group(0, 0)
            with pe.Fori(0, LOOPED // 2) as i:
                for s in (1, 0):
                    next_edges(i * 2 + 5 - s, 1 - s)
                    next_pick(i * 2 + 4 - s, s)
                    group(i * 2 + 2 - s, s)
            for g in range(LOOPED + 1, LATE - 1):
                next_edges(g + 3, (g + 1) % 2, whole=g + 3 < LAST)
                next_pick(g + 2, g % 2)
                group(g, g % 2)
            pe.wait_ge(last_filled, LAST)
            pe.wait_ge(w2_in, 32)
            for n in range(U_EARLY):
                own_part(n)
            group(LATE - 1, LAST % 2)
            for n in range(U_EARLY, U_MIDDLE):
                own_part(n)
            more = {g: windows_beyond(g) for g in (LATE, LAST)}
            pe.wait_ge(filled, GROUPS)
            for n, (g, tiles) in enumerate(((LATE, TPG), (LAST, LAST_TILES))):
                pe.wait_ge(hot_ready, g + 1)
                edge_counts(count_ps[n], hot[:, g % 2], tiles).then_inc(counts_ready, 1)
                extra_windows(more[g], lambda: edge_counts(count_x[n], hot_x, tiles))
            for n in range(U_MIDDLE, U_STEPS):
                own_part(n)
            pe.wait_ge(all_counted, 1)
            for t in range(TILES):
                last = nc.tensor.transpose(degree_cols[:, t:t + 1], sums[0:1, 1, t * P:(t + 1) * P], ident[0:1, 0:1])
            last.then_inc(degree_ps, 1)
            for g, tiles in ((LATE, TPG), (LAST, LAST_TILES)):
                pe.wait_ge(parts_ready, g + 1)
                message_sums(sum_ps[g % 2], g % 2, hot[:, g % 2], tiles).then_inc(sums_ready, 1)
                extra_windows(more[g], lambda: message_sums(late_x[g % 2], g % 2, hot_x, tiles))
            pe.wait_ge(summed, GROUPS + SLOT_CREDIT)
            pe.wait_ge(inv_done, 1)
            for n in range(OUT_STEPS):
                for t in range(*out_tiles(n)):
                    last = nc.tensor.matmul(out_ps(n)[:, t % OUT_TILES, :], sums[:, 0, t * P:(t + 1) * P], w2b_sb[:, :],
                                            start=True, stop=True)
                last.then_inc(fin_ps, 1)


def kernel(x, src, dst, edge_attr_3, L0_gnn_W1, L0_gnn_W2, L0_gnn_b2):
    import concourse.bacc as bacc
    from concourse import mybir
    from concourse.bass_utils import run_bass_kernel_spmd

    x, src, dst, edge = (np.asarray(a) for a in (x, src, dst, edge_attr_3))
    w1, w2, b2 = (np.asarray(a) for a in (L0_gnn_W1, L0_gnn_W2, L0_gnn_b2))
    src_pad = np.zeros((LAST_STAGED + 1) * GROUP, src.dtype)
    src_pad[:EDGES] = src
    dst_pad = np.full(GROUPS * GROUP, NODES, dst.dtype)
    dst_pad[:EDGES] = dst
    edge_pad = np.zeros((GROUPS * GROUP, EDIM), edge.dtype)
    edge_pad[:EDGES] = edge
    edge_rows = edge_pad.reshape(GROUPS, TPG, P, EDIM).transpose(0, 1, 3, 2).reshape(GROUPS, KE, P)
    w1b_rows = np.zeros((KE, TPG * F), w1.dtype)
    for t in range(TPG):
        w1b_rows[t * EDIM:(t + 1) * EDIM, t * F:(t + 1) * F] = w1[:, F:].T
    signs = np.zeros((KS, 4), np.float32)
    for n, (e, w) in enumerate(PAIRS):
        signs[n * KE:(n + 1) * KE] = [-(e > 0), -(e > 1), -(w > 0), -(w > 1)]
    arrays = {
        "x": x,
        "src_cols": np.ascontiguousarray(src_pad.reshape(-1, P).T),
        "src_last": np.ascontiguousarray(src_pad[:GROUPS * GROUP].reshape(GROUPS, TPG, P)[:, TPG - 1]),
        "dst_cols": np.ascontiguousarray(dst_pad.reshape(-1, P).T),
        "dst_rows": dst_pad.reshape(GROUPS, GROUP),
        "edge_rows": np.tile(edge_rows, (1, len(PAIRS), 1)),
        "split_signs": signs,
        "w1a": np.ascontiguousarray(w1[:, :F].T),
        "w1b_rows": np.tile(w1b_rows, (len(PAIRS), 1)),
        "w2a": np.ascontiguousarray(w2[:, :F].T),
        "w2b": np.ascontiguousarray(w2[:, F:].T),
        "b2": b2.reshape(1, F),
    }
    nc = bacc.Bacc("TRN2", target_bir_lowering=False, num_devices=1)
    args = [nc.dram_tensor(k, a.shape, mybir.dt.from_np(a.dtype), kind="ExternalInput").ap() for k, a in arrays.items()]
    proj = nc.dram_tensor("proj", (NPAD, F), mybir.dt.float32, kind="Internal").ap()
    src_narrow = nc.dram_tensor("src_narrow", (GROUPS, P), mybir.dt.int16, kind="Internal").ap()
    out = nc.dram_tensor("out", (NODES, F), mybir.dt.float32, kind="ExternalOutput").ap()
    build(nc, *args, proj, src_narrow, out)
    result = run_bass_kernel_spmd(nc, [arrays], core_ids=[0])
    return result.results[0]["out"]
```
